# Optimizing a Trainium2 kernel written in Bass

```python
import numpy as np
import jax
import jax.numpy as jnp

def _softmax(x, axis=-1):
    return jax.nn.softmax(x, axis=axis)

def _gelu(x):
    return jax.nn.gelu(x, approximate=True)

def _silu(x):
    return jax.nn.silu(x)

def _sigmoid(x):
    return jax.nn.sigmoid(x)

def _layernorm(x, axis=-1, eps=1e-05):
    m = jnp.mean(x, axis=axis, keepdims=True)
    v = jnp.var(x, axis=axis, keepdims=True)
    return (x - m) / jnp.sqrt(v + eps)

def _scatter_add(tgt, idx, src, axis=0):
    return tgt.at[idx].add(src)

def _segment_sum(src, seg, n):
    return jax.ops.segment_sum(src, seg, n)
kernel_name = 'mk_macaron_d1_jaxref_r8_2928b3'

def setup_inputs(seed: int=0):
    np.random.seed(seed)
    _w = jnp.asarray

    def _L0_attn_setup():
        import jax, jax.numpy as jnp
        import numpy as np
        B, L, D, H = (2, 256, 128, 4)
        DV = D // H
        P = 5
        CHUNK = 32
        CONV_K = 4
        FIR_K = (3, 15, 64)

        def _dwconv(x, w):
            K = w.shape[1]
            xt = jnp.pad(jnp.transpose(x, (0, 2, 1)), ((0, 0), (0, 0), (K - 1, 0)))
            y = jax.lax.conv_general_dilated(xt, w[:, None, :], (1,), 'VALID', dimension_numbers=('NCH', 'OIH', 'NCH'), feature_group_count=w.shape[0])
            return jnp.transpose(y, (0, 2, 1))

        def _l2norm(x):
            return x * jax.lax.rsqrt(jnp.sum(x * x, -1, keepdims=True) + 1e-06)

        def _delta_rule_chunkwise(q, k, v, beta, chunk=CHUNK):
            b, h, Lp, dk = q.shape
            dv = v.shape[-1]
            n = Lp // chunk
            q = _l2norm(q)
            k = _l2norm(k)
            v = v * beta[..., None]
            kb = k * beta[..., None]
            r = lambda t: t.reshape(b, h, n, chunk, -1)
            q, k, v, kb = (r(q), r(k), r(v), r(kb))
            sw = lambda t: jnp.swapaxes(t, -1, -2)
            strict = jnp.tril(jnp.ones((chunk, chunk), bool), -1)
            attn = jnp.where(strict, -(kb @ sw(k)), 0.0)
            T = jnp.linalg.inv(jnp.eye(chunk, dtype=q.dtype) - attn)
            u = T @ v
            w = T @ kb
            incl = jnp.tril(jnp.ones((chunk, chunk), bool), 0)
            qs, ks, us, ws = (jnp.moveaxis(t, 2, 0) for t in (q, k, u, w))
            S0 = jnp.zeros((b, h, dk, dv), q.dtype)

            def step(S, inp):
                q_i, k_i, u0, w_i = inp
                local = jnp.where(incl, q_i @ sw(k_i), 0.0)
                u_i = u0 - w_i @ S
                o_i = q_i @ S + local @ u_i
                return (S + sw(k_i) @ u_i, o_i)
            S, o = jax.lax.scan(step, S0, (qs, ks, us, ws))
            return (jnp.moveaxis(o, 0, 2).reshape(b, h, Lp, dv), S)

        def _stats(t):
            m = jnp.mean(t, -1, keepdims=True)
            v = jnp.mean(t * t, -1, keepdims=True)
            a = jnp.mean(jnp.abs(t), -1, keepdims=True)
            nrm = jnp.sqrt(jnp.sum(t * t, -1, keepdims=True))
            s = jnp.concatenate([jnp.broadcast_to(x, t.shape) for x in (m, v, a, nrm)], -1)
            return s.reshape(t.shape[0], t.shape[1], -1)

        def _forward(hs, Wq, Wk, Wv, conv_q, conv_k, conv_v, Wb, fir_s, fir_m, fir_l, gW1, gb1, gW2, gb2, log_tau, eps_logit, norm_w, Wo):
            b, Ln, _ = hs.shape
            q = jax.nn.silu(_dwconv(hs @ Wq, conv_q))
            k = jax.nn.silu(_dwconv(hs @ Wk, conv_k))
            v = jax.nn.silu(_dwconv(hs @ Wv, conv_v))
            beta = jax.nn.sigmoid(hs @ Wb)
            bh = lambda t: jnp.transpose(t.reshape(b, Ln, H, -1), (0, 2, 1, 3))
            o_d, _ = _delta_rule_chunkwise(bh(q), bh(k), bh(v), jnp.transpose(beta, (0, 2, 1)))
            delta_path = jnp.transpose(o_d, (0, 2, 1, 3))
            paths = jnp.stack([_dwconv(v, fir_s).reshape(b, Ln, H, DV), _dwconv(v, fir_m).reshape(b, Ln, H, DV), _dwconv(v, fir_l).reshape(b, Ln, H, DV), delta_path, v.reshape(b, Ln, H, DV)], axis=3)
            stats_flat = jnp.concatenate([_stats(paths[..., p, :]) for p in range(P)], -1)
            gate_in = jnp.concatenate([hs, stats_flat], -1)
            logits = jax.nn.gelu(gate_in @ gW1 + gb1, approximate=False) @ gW2 + gb2
            logits = logits.reshape(b, Ln, H, P)
            tau = jax.nn.softplus(log_tau) + 0.5
            probs = jax.nn.softmax(logits / tau[:, None], -1)
            eps = jax.nn.sigmoid(eps_logit) * 0.2
            probs = probs * (1.0 - jnp.sum(eps, -1, keepdims=True)) + eps
            o = jnp.einsum('blhp,blhpd->blhd', probs, paths)
            o = o * jax.lax.rsqrt(jnp.mean(o * o, -1, keepdims=True) + 1e-05) * norm_w
            return o.reshape(b, Ln, D) @ Wo
        key = jax.random.key(seed)
        ks = jax.random.split(key, 14)
        lin = lambda kk, fan_in, shape: jax.random.normal(kk, shape, jnp.float32) / np.float32(np.sqrt(fan_in))

        def fir(kk, K):
            w = np.zeros((D, K), np.float32)
            w[:, -1] = 1.0
            return jnp.asarray(w) + 0.001 * jax.random.normal(kk, (D, K), jnp.float32)
        in_gate = D + 4 * DV * H * P
        HF = 2 * D
        gb2 = np.zeros((H * P,), np.float32)
        gb2[np.arange(H) * P + P - 1] = 1.0
        return {'hidden_states': jax.random.normal(ks[0], (B, L, D), jnp.float32), 'Wq': lin(ks[1], D, (D, D)), 'Wk': lin(ks[2], D, (D, D)), 'Wv': lin(ks[3], D, (D, D)), 'conv_q': lin(ks[4], CONV_K, (D, CONV_K)), 'conv_k': lin(ks[5], CONV_K, (D, CONV_K)), 'conv_v': lin(ks[6], CONV_K, (D, CONV_K)), 'Wb': lin(ks[7], D, (D, H)), 'fir_s': fir(ks[8], FIR_K[0]), 'fir_m': fir(ks[9], FIR_K[1]), 'fir_l': fir(ks[10], FIR_K[2]), 'gW1': lin(ks[11], in_gate, (in_gate, HF)), 'gb1': jnp.zeros((HF,), jnp.float32), 'gW2': lin(ks[12], HF, (HF, H * P)), 'gb2': jnp.asarray(gb2), 'log_tau': jnp.zeros((H,), jnp.float32), 'eps_logit': jnp.zeros((H, P), jnp.float32), 'norm_w': jnp.ones((DV,), jnp.float32), 'Wo': lin(ks[13], D, (D, D))}
    _L0_attn_in = _L0_attn_setup()

    def _L0_ffn_setup():
        import jax, jax.numpy as jnp
        import numpy as np
        D_IN, D_HID = (128, 512)

        def _ternary(key, shape):
            return jax.random.randint(key, shape, -1, 2).astype(jnp.float32)

        def _tlin(x, w, s):
            return jnp.einsum('bsi,oi->bso', x, w) * s
        key = jax.random.key(seed)
        ks = jax.random.split(key, 12)
        inv = lambda fan: 1.0 / np.sqrt(fan).astype(np.float32)
        return {'x': jax.random.normal(ks[0], (4, 256, D_IN), dtype=jnp.float32), 'w1_w': _ternary(ks[1], (D_HID, D_IN)), 'w1_s': jax.random.uniform(ks[2], (D_HID,), dtype=jnp.float32) * inv(D_IN), 'w2_w': _ternary(ks[3], (D_HID, D_IN)), 'w2_s': jax.random.uniform(ks[4], (D_HID,), dtype=jnp.float32) * inv(D_IN), 'h1_w': _ternary(ks[5], (D_HID, D_HID)), 'h1_s': jax.random.uniform(ks[6], (D_HID,), dtype=jnp.float32) * inv(D_HID), 'h2_w': _ternary(ks[7], (D_HID, D_HID)), 'h2_s': jax.random.uniform(ks[8], (D_HID,), dtype=jnp.float32) * inv(D_HID), 'w3_w': _ternary(ks[9], (D_IN, D_HID)), 'w3_s': jax.random.uniform(ks[10], (D_IN,), dtype=jnp.float32) * inv(D_HID)}
    _L0_ffn_in = _L0_ffn_setup()
    _d = {'L0_attn_hidden_states': _L0_attn_in['hidden_states'], 'L0_attn_Wq': _L0_attn_in['Wq'], 'L0_attn_Wk': _L0_attn_in['Wk'], 'L0_attn_Wv': _L0_attn_in['Wv'], 'L0_attn_conv_q': _L0_attn_in['conv_q'], 'L0_attn_conv_k': _L0_attn_in['conv_k'], 'L0_attn_conv_v': _L0_attn_in['conv_v'], 'L0_attn_Wb': _L0_attn_in['Wb'], 'L0_attn_fir_s': _L0_attn_in['fir_s'], 'L0_attn_fir_m': _L0_attn_in['fir_m'], 'L0_attn_fir_l': _L0_attn_in['fir_l'], 'L0_attn_gW1': _L0_attn_in['gW1'], 'L0_attn_gb1': _L0_attn_in['gb1'], 'L0_attn_gW2': _L0_attn_in['gW2'], 'L0_attn_gb2': _L0_attn_in['gb2'], 'L0_attn_log_tau': _L0_attn_in['log_tau'], 'L0_attn_eps_logit': _L0_attn_in['eps_logit'], 'L0_attn_norm_w': _L0_attn_in['norm_w'], 'L0_attn_Wo': _L0_attn_in['Wo'], 'L0_ffn_w1_w': _L0_ffn_in['w1_w'], 'L0_ffn_w1_s': _L0_ffn_in['w1_s'], 'L0_ffn_w2_w': _L0_ffn_in['w2_w'], 'L0_ffn_w2_s': _L0_ffn_in['w2_s'], 'L0_ffn_h1_w': _L0_ffn_in['h1_w'], 'L0_ffn_h1_s': _L0_ffn_in['h1_s'], 'L0_ffn_h2_w': _L0_ffn_in['h2_w'], 'L0_ffn_h2_s': _L0_ffn_in['h2_s'], 'L0_ffn_w3_w': _L0_ffn_in['w3_w'], 'L0_ffn_w3_s': _L0_ffn_in['w3_s']}
    _x0 = _d['L0_attn_hidden_states']
    _d['L0_attn_hidden_states'] = jax.random.normal(jax.random.fold_in(jax.random.key(seed), 1), (8, 256, 128), dtype=_x0.dtype)
    del _x0
    return _d

def reference(L0_attn_hidden_states, L0_attn_Wq, L0_attn_Wk, L0_attn_Wv, L0_attn_conv_q, L0_attn_conv_k, L0_attn_conv_v, L0_attn_Wb, L0_attn_fir_s, L0_attn_fir_m, L0_attn_fir_l, L0_attn_gW1, L0_attn_gb1, L0_attn_gW2, L0_attn_gb2, L0_attn_log_tau, L0_attn_eps_logit, L0_attn_norm_w, L0_attn_Wo, L0_ffn_w1_w, L0_ffn_w1_s, L0_ffn_w2_w, L0_ffn_w2_s, L0_ffn_h1_w, L0_ffn_h1_s, L0_ffn_h2_w, L0_ffn_h2_s, L0_ffn_w3_w, L0_ffn_w3_s):

    def _L0_attn_ref(hidden_states, Wq, Wk, Wv, conv_q, conv_k, conv_v, Wb, fir_s, fir_m, fir_l, gW1, gb1, gW2, gb2, log_tau, eps_logit, norm_w, Wo):
        import jax, jax.numpy as jnp
        import numpy as np
        B, L, D, H = (2, 256, 128, 4)
        DV = D // H
        P = 5
        CHUNK = 32
        CONV_K = 4
        FIR_K = (3, 15, 64)

        def _dwconv(x, w):
            K = w.shape[1]
            xt = jnp.pad(jnp.transpose(x, (0, 2, 1)), ((0, 0), (0, 0), (K - 1, 0)))
            y = jax.lax.conv_general_dilated(xt, w[:, None, :], (1,), 'VALID', dimension_numbers=('NCH', 'OIH', 'NCH'), feature_group_count=w.shape[0])
            return jnp.transpose(y, (0, 2, 1))

        def _l2norm(x):
            return x * jax.lax.rsqrt(jnp.sum(x * x, -1, keepdims=True) + 1e-06)

        def _delta_rule_chunkwise(q, k, v, beta, chunk=CHUNK):
            b, h, Lp, dk = q.shape
            dv = v.shape[-1]
            n = Lp // chunk
            q = _l2norm(q)
            k = _l2norm(k)
            v = v * beta[..., None]
            kb = k * beta[..., None]
            r = lambda t: t.reshape(b, h, n, chunk, -1)
            q, k, v, kb = (r(q), r(k), r(v), r(kb))
            sw = lambda t: jnp.swapaxes(t, -1, -2)
            strict = jnp.tril(jnp.ones((chunk, chunk), bool), -1)
            attn = jnp.where(strict, -(kb @ sw(k)), 0.0)
            T = jnp.linalg.inv(jnp.eye(chunk, dtype=q.dtype) - attn)
            u = T @ v
            w = T @ kb
            incl = jnp.tril(jnp.ones((chunk, chunk), bool), 0)
            qs, ks, us, ws = (jnp.moveaxis(t, 2, 0) for t in (q, k, u, w))
            S0 = jnp.zeros((b, h, dk, dv), q.dtype)

            def step(S, inp):
                q_i, k_i, u0, w_i = inp
                local = jnp.where(incl, q_i @ sw(k_i), 0.0)
                u_i = u0 - w_i @ S
                o_i = q_i @ S + local @ u_i
                return (S + sw(k_i) @ u_i, o_i)
            S, o = jax.lax.scan(step, S0, (qs, ks, us, ws))
            return (jnp.moveaxis(o, 0, 2).reshape(b, h, Lp, dv), S)

        def _stats(t):
            m = jnp.mean(t, -1, keepdims=True)
            v = jnp.mean(t * t, -1, keepdims=True)
            a = jnp.mean(jnp.abs(t), -1, keepdims=True)
            nrm = jnp.sqrt(jnp.sum(t * t, -1, keepdims=True))
            s = jnp.concatenate([jnp.broadcast_to(x, t.shape) for x in (m, v, a, nrm)], -1)
            return s.reshape(t.shape[0], t.shape[1], -1)

        def _forward(hs, Wq, Wk, Wv, conv_q, conv_k, conv_v, Wb, fir_s, fir_m, fir_l, gW1, gb1, gW2, gb2, log_tau, eps_logit, norm_w, Wo):
            b, Ln, _ = hs.shape
            q = jax.nn.silu(_dwconv(hs @ Wq, conv_q))
            k = jax.nn.silu(_dwconv(hs @ Wk, conv_k))
            v = jax.nn.silu(_dwconv(hs @ Wv, conv_v))
            beta = jax.nn.sigmoid(hs @ Wb)
            bh = lambda t: jnp.transpose(t.reshape(b, Ln, H, -1), (0, 2, 1, 3))
            o_d, _ = _delta_rule_chunkwise(bh(q), bh(k), bh(v), jnp.transpose(beta, (0, 2, 1)))
            delta_path = jnp.transpose(o_d, (0, 2, 1, 3))
            paths = jnp.stack([_dwconv(v, fir_s).reshape(b, Ln, H, DV), _dwconv(v, fir_m).reshape(b, Ln, H, DV), _dwconv(v, fir_l).reshape(b, Ln, H, DV), delta_path, v.reshape(b, Ln, H, DV)], axis=3)
            stats_flat = jnp.concatenate([_stats(paths[..., p, :]) for p in range(P)], -1)
            gate_in = jnp.concatenate([hs, stats_flat], -1)
            logits = jax.nn.gelu(gate_in @ gW1 + gb1, approximate=False) @ gW2 + gb2
            logits = logits.reshape(b, Ln, H, P)
            tau = jax.nn.softplus(log_tau) + 0.5
            probs = jax.nn.softmax(logits / tau[:, None], -1)
            eps = jax.nn.sigmoid(eps_logit) * 0.2
            probs = probs * (1.0 - jnp.sum(eps, -1, keepdims=True)) + eps
            o = jnp.einsum('blhp,blhpd->blhd', probs, paths)
            o = o * jax.lax.rsqrt(jnp.mean(o * o, -1, keepdims=True) + 1e-05) * norm_w
            return o.reshape(b, Ln, D) @ Wo
        return _forward(hidden_states, Wq, Wk, Wv, conv_q, conv_k, conv_v, Wb, fir_s, fir_m, fir_l, gW1, gb1, gW2, gb2, log_tau, eps_logit, norm_w, Wo)

    def _L0_ffn_ref(x, w1_w, w1_s, w2_w, w2_s, h1_w, h1_s, h2_w, h2_s, w3_w, w3_s):
        import jax, jax.numpy as jnp
        import numpy as np
        D_IN, D_HID = (128, 512)

        def _ternary(key, shape):
            return jax.random.randint(key, shape, -1, 2).astype(jnp.float32)

        def _tlin(x, w, s):
            return jnp.einsum('bsi,oi->bso', x, w) * s
        h = jax.nn.silu(_tlin(x, w1_w, w1_s)) * _tlin(x, w2_w, w2_s)
        h = jax.nn.gelu(_tlin(h, h1_w, h1_s), approximate=False)
        h = jax.nn.gelu(_tlin(h, h2_w, h2_s), approximate=False)
        return _tlin(h, w3_w, w3_s)
    x = L0_attn_hidden_states
    x = x + 0.5 * _L0_ffn_ref(_layernorm(x, axis=-1), L0_ffn_w1_w, L0_ffn_w1_s, L0_ffn_w2_w, L0_ffn_w2_s, L0_ffn_h1_w, L0_ffn_h1_s, L0_ffn_h2_w, L0_ffn_h2_s, L0_ffn_w3_w, L0_ffn_w3_s)
    x = x + _L0_attn_ref(_layernorm(x, axis=-1), L0_attn_Wq, L0_attn_Wk, L0_attn_Wv, L0_attn_conv_q, L0_attn_conv_k, L0_attn_conv_v, L0_attn_Wb, L0_attn_fir_s, L0_attn_fir_m, L0_attn_fir_l, L0_attn_gW1, L0_attn_gb1, L0_attn_gW2, L0_attn_gb2, L0_attn_log_tau, L0_attn_eps_logit, L0_attn_norm_w, L0_attn_Wo)
    x = x + 0.5 * _L0_ffn_ref(_layernorm(x, axis=-1), L0_ffn_w1_w, L0_ffn_w1_s, L0_ffn_w2_w, L0_ffn_w2_s, L0_ffn_h1_w, L0_ffn_h1_s, L0_ffn_h2_w, L0_ffn_h2_s, L0_ffn_w3_w, L0_ffn_w3_s)
    return x

_drawn_inputs = setup_inputs


def setup_inputs(seed=0):
    import zlib

    import numpy as np

    out = dict(_drawn_inputs(seed))
    spreads = {'L0_attn_gb1': (0.0, 0.1),
     'L0_attn_log_tau': (0.0, 0.1),
     'L0_attn_eps_logit': (0.0, 0.1),
     'L0_attn_norm_w': (1.0, 0.2)}
    factors = {}
    for name, (base, spread) in spreads.items():
        noise = np.random.default_rng([zlib.crc32(name.encode()), seed]).standard_normal(out[name].shape)
        drawn = base * np.exp(spread * noise) if base else spread * noise
        out[name] = jnp.asarray(drawn.astype(out[name].dtype))
    for name, factor in factors.items():
        out[name] = (out[name] * factor).astype(out[name].dtype)
    return out
```

```python
from contextlib import ExitStack

import concourse.bass as bass
from concourse import mybir

ALU = mybir.AluOpType
ACT = mybir.ActivationFunctionType
AX_X = mybir.AxisListType.X
F32 = mybir.dt.float32
F32R = mybir.dt.float32r

B, L, D, H, P = 8, 256, 128, 4, 5
DH = D // H
HID = 512
KT = HID // 128
TILE = 512
NT = B * L // TILE
NCH = L // DH
TAPS = 4
PAD = 4
HIST, WIN = 64, 96
LN_EPS, L2_EPS, RMS_EPS = 1e-5, 1e-6, 1e-5
NRING = 4

def ffn_steps(f):
    s = []
    for a in range(0, NT, 2):
        b = a + 1
        if a == 0:
            s += [("in", f, 0), ("in", f, 1)] if f == 0 else []
            s += [("mean", f, 0), ("mean", f, 1), ("var", f, 0), ("var", f, 1)]
        more = a + 2 < NT
        s += [("up", f, a), ("up", f, b)]
        if more and f == 0:
            s += [("in", f, a + 2), ("in", f, b + 2)]
        if more:
            s += [("mean", f, a + 2), ("mean", f, b + 2)]
        s += [("hid1", f, a), ("hid1", f, b)]
        if more:
            s += [("var", f, a + 2), ("var", f, b + 2)]
        s += [("hid2", f, a), ("hid2", f, b), ("down", f, a), ("down", f, b)]
        if f == 1:
            s += [("out", f, a), ("out", f, b)]
    return s


def att_steps():
    s = [("mean", 2, 0), ("mean", 2, 1), ("var", 2, 0), ("var", 2, 1)]
    for t in range(NT):
        s.append(("qkv", 2, t))
        if t + 2 < NT:
            s += [("mean", 2, t + 2), ("var", 2, t + 2)]
        if t:
            s.append(("sumsq", 2, t - 1))
    s.append(("sumsq", 2, NT - 1))
    s += [("vpath", 2, 0)]
    s += [("window", 2, i) for i in range(16)]
    s += [("token", 2, i) for i in range(12)]
    s += [("gram", 2, g) for g in range(2)]
    s += [("inverse", 2, 0)]
    s += [("fir", 2, i) for i in range(16)]
    s += [("chain", 2, n) for n in range(NCH)]
    s += [("stats", 2, 0)]
    for t in range(NT):
        s += [("gate", 2, t), ("logit", 2, t)]
    s += [("mix", 2, 0)]
    s += [("wo", 2, t) for t in range(NT)]
    return s


STEPS = ffn_steps(0) + att_steps() + ffn_steps(1)

RING_A = {"in": 1, "up": KT, "hid1": KT, "hid2": KT, "out": 1, "qkv": 4, "fir": 1, "gate": 2}
RING_D = {"mean": 1, "var": 1, "up": KT, "down": 1, "sumsq": 2, "gram": H, "logit": 1, "wo": 1}


def ring_of(step):
    kind, _, i = step
    if kind in ("window", "token"):
        return (1, 0) if i % 2 == 0 else (0, 1)
    return RING_A.get(kind, 0), RING_D.get(kind, 0)


def before(kinds, weight=lambda s: 1):
    out, n = {}, 0
    for s in STEPS:
        out[s] = n
        if s[0] in kinds:
            n += weight(s)
    return out, n


ANY = {s[0] for s in STEPS}
A_AT, A_ALL = before(ANY, lambda s: ring_of(s)[0])
D_AT, D_ALL = before(ANY, lambda s: ring_of(s)[1])
LAYERS = ("up", "hid1", "hid2")
SET_AT, _ = before(LAYERS)
USED_AT, _ = before(("hid1", "hid2", "down"))
USERS = [s for s in STEPS if s[0] in ("hid1", "hid2", "down")]
NORM_AT, _ = before(("mean",))
VAR_AT, _ = before(("var",))

STAT_ORDER = (4, 0, 1, 2, 3)

V = dict(s1=0, s2=4, g1=8, g2=12, s3=16, norm=17, ltau=18, gb2=19, gb1=20, epsl=22, share=27,
         atau=28, etau=29, eeps=30, lntau=35, s3h=36, itau=37, eps=38, rest=43, l2eps=44, lneps=45, rmseps=46,
         mtau=47, epsd=48)
NVEC = 28

ARENA = 38800
AO = dict(tinv=0, lmat=2048, tmp=4096, vt=5632, kq=13824, ktok=17920, vtok=19968,
          alt=22016, vpad=22016, paths=26112, kn=26112, vb=28160, ln=30208, kbtok=32256, ny=35328, u=37376,
          block=0, sq=4096, ssb=6144, st=8192, ot=10240, uexp=12288, wt=13312,
          stt=0, hid=2048, lg=4096, pl=6144, mix=0, o=2048, oc=8192, small=12288)


def program(nc, d, out):
    ctx = ExitStack()
    with ctx:
        def sb(name, shape, dt=F32, c=ctx):
            return c.enter_context(nc.sbuf_tensor(name, shape, dt))

        def sem(name):
            return ctx.enter_context(nc.semaphore(name))

        ps_a = [ctx.enter_context(nc.psum_tensor(f"ps_a{i}", [128, 512], F32)) for i in range(NRING)]
        ps_d = ctx.enter_context(nc.psum_tensor("ps_d", [128, NRING, 512], F32))

        x_t = sb("x_t", [128, B * L])
        ident = sb("ident", [128, 128])
        mean_w = sb("mean_w", [128, 128])
        head_w = sb("head_w", [128, 128])
        mask = sb("mask", [128, 2, DH])
        gate_x = sb("gate_x", [128, 2, 2 * D], F32R)
        gate_s = sb("gate_s", [128, 2 * D])
        gate_2 = sb("gate_2", [128, 2, 128])
        wo_w = sb("wo_w", [128, D])
        vec = sb("vec", [128, 56])
        toep = sb("toep", [128, 2, H, 8, WIN])

        c1 = ExitStack()
        w_f = [sb("w_f0", [128, 5632], F32R, c1)]
        conv_w = sb("conv_w", [128, 2, 13, 128], F32R, c1)
        acts = [sb("acts0", [128, 3, 2, KT, TILE], F32R, c1)]
        xn_f = [sb("xn0", [128, 2, 2, TILE], F32R, c1)]
        fwork = [sb("fwork0", [128, 10240], F32, c1)]
        gtmp = sb("gtmp", [128, 8192], F32, c1)
        c1.close()
        c2 = ExitStack()
        arena = sb("arena", [128, ARENA], F32, c2)
        xnp = sb("xnp", [128, 2, B, PAD + L], F32R, c2)
        c2.close()
        c3 = ExitStack()
        acts.append(sb("acts1", [128, 3, 2, KT, TILE], F32R, c3))
        spare = sb("spare", [128, AO["kq"] - 12288], F32, c3)
        w_f.append(sb("w_f1", [128, 5632], F32R, c3))
        wstage = sb("wstage1", [128, 5632], F32, c3)
        xn_f.append(sb("xn1", [128, 2, 2, TILE], F32R, c3))
        fwork.append(sb("fwork1", [128, 10240], F32, c3))
        c3.close()

        def at(name, *shape):
            n = 1
            for s in shape:
                n *= s
            v = arena[:, AO[name]:AO[name] + n]
            if len(shape) == 1:
                return v
            names = "abcdef"[:len(shape)]
            return v.rearrange(f"p ({' '.join(names)}) -> p {' '.join(names)}", **dict(zip(names, shape)))

        def ln_bufs(f):
            v = at("ln", 10, TILE) if f == 2 else fwork[f][:, 0:5120].rearrange("p (a b) -> p a b", a=10)
            return {k: v[:, 2 * i:2 * i + 2, :] for i, k in enumerate(("xc", "sq", "y", "t3", "u"))}

        gbuf = [w[:, 5120:7168].rearrange("p (a b) -> p a b", a=4) for w in fwork]
        hbuf = [w[:, 7168:8192].rearrange("p (a b) -> p a b", a=2) for w in fwork]
        iobuf = [w[:, 8192:10240].rearrange("p (a j c) -> p a j c", a=4, j=4) for w in fwork]

        kq = at("kq", 2, 16, 128)
        kn = at("kn", 16, 128)
        vb = at("vb", 16, 128)
        vpad = at("vpad", B, HIST + L)
        vt = at("vt", 128, 2, 32)
        ktok = at("ktok", 16, 128)
        vtok = at("vtok", 16, 128)
        alt = at("alt", 2, H, NCH, 2, DH)
        lmat = at("lmat", 2, DH, DH)
        tinv = at("tinv", 2, DH, DH)
        tmp = at("tmp", 1024)
        block = at("block", 2, 8, 2, 128)
        paths = [at("paths", P, 64, DH)[:, p] for p in range(P)]
        kbtok = at("kbtok", 16, 128)
        s_sb = at("ssb", 2, B, 128)
        u_exp = at("uexp", 2, 4, 128)
        u_sb = at("u", 2, 128)
        w_t = at("wt", 2, 2, 128)
        o_t = at("ot", B * L)
        sq_p = at("sq", 2, 32, DH)
        st = at("st", 64, 32)
        st_t = at("stt", B * L)
        hid = at("hid", 2, 2, TILE)
        lg = at("lg", B * L)
        pl = at("pl", 64, 32)
        mixt = at("mix", 64, DH)
        o_p = at("o", 64, DH)
        o_c = at("oc", B * L)
        sm = at("small", 1536)
        qs = at("tinv", 10, TILE)

        names = ("ld_x ld_x2 ld_up ld_hid ld_vec ld_proj ld_gate ld_late ld_w2 ld_t0 ld_t1 st_out "
                 "consts mask_done up_round hid_round conv_round gate_sum w2_round vec_act vec_dve "
                 "pe_a act_a pe_d dve_d dve_lo act_sq act_t dve_xn pad_zero "
                 "act_ss act_nt dve_nrm eye_done inv_done block_zero act_block pe_p dve_u act_u pe_w act_w pe_o act_o "
                 "pe_s dve_s st_zero act_stat dve_stat act_norm path3 st_turned act_exp dve_sub dve_o act_osq dve_ms act_rms "
                 "o_turned dve_step act_step pool_step").split()
        S = {n: sem(n) for n in names}
        x_dram = d["x"].rearrange("(a j p) c -> a p j c", j=4, p=128)
        out_dram = out.rearrange("(a j p) c -> a p j c", j=4, p=128)
        wst1 = gtmp[:, 0:5632]
        tflat = toep[:, :, :, :, :].rearrange("p a h d x -> p (a h d x)")
        taps = tflat[:, 0:1536]
        proj = tflat[:, 1536:2048].rearrange("p (i n) -> p i n", i=4)
        conv_s = tflat[:, 2048:2048 + 13 * 128].rearrange("p (i n) -> p i n", i=13)
        gx_s = tflat[:, 3712:3968]
        mtmp = tflat[:, 3968:4224].rearrange("p (a b) -> p a b", a=2)
        lnb = {f: ln_bufs(f) for f in range(3)}
        ny = at("ny", 4, TILE)
        pall = at("paths", P, 64, DH)

        def vc(name, i=0, n=1):
            return vec[:, V[name] + i:V[name] + i + n]

        def tile(ap, t):
            return ap[:, t * TILE:(t + 1) * TILE]

        def chunked(ap, t):
            g, o = t // 2, 64 * (t % 2)
            return ap[:, NCH * g:NCH * g + NCH, o:o + 64].rearrange("p n (b t) -> p b n t", b=2)

        def plain(ap):
            return ap.rearrange("p (b n t) -> p b n t", b=2, n=NCH)

        def x_ready(e, f, t):
            if f == 0:
                e.wait_ge(S["act_a"], A_AT[("in", 0, t)] + 1)
            elif f == 2:
                e.wait_ge(S["dve_d"], D_AT[("down", 0, t)] + 1)
            else:
                e.wait_ge(S["dve_d"], D_AT[("wo", 2, t)] + 1)

        def part_entry(e, f):
            if f == 2:
                e.wait_ge(S["dve_d"], D_AT[("down", 0, NT - 1)] + 1)
                e.wait_ge(S["gate_sum"], 1)
                e.wait_ge(S["conv_round"], 1)
            if f == 1:
                e.wait_ge(S["dve_d"], D_AT[("wo", 2, NT - 1)] + 1)

        def set_free(e, j):
            if j >= 3:
                user = USERS[j - 3]
                if user[0] == "down":
                    e.wait_ge(S["pe_d"], D_AT[user] + 1)
                else:
                    e.wait_ge(S["pe_a"], A_AT[user] + KT)

        ENTRY = {("mean", 2, 0): 2, ("mean", 1, 0): 1}

        def load_weights(e, stage, first, rest):
            e.dma_start(stage[:, 0:512], d["w1"]).then_inc(first, 16)
            e.dma_start(stage[:, 512:1024], d["w2"]).then_inc(first, 16)
            for k, o in (("h1", 1024), ("h2", 3072)):
                e.dma_start(stage[:, o:o + 2048].rearrange("p (k n) -> p k n", k=KT),
                            d[k].rearrange("(k p) n -> p k n", p=128)).then_inc(rest, 16)
            e.dma_start(stage[:, 5120:5632].rearrange("p (k n) -> p k n", k=KT),
                        d["w3"].rearrange("(k p) n -> p k n", p=128)).then_inc(rest, 16)

        def load_toep(e, grp):
            for h in range(H):
                src = d["fir"][h * DH + 8 * grp:h * DH + 8 * grp + 8, :]
                rows = bass.AP(src.tensor, src.offset, [[3, WIN], [384, 8], [1, WIN]])
                e.dma_start(toep[0:WIN, grp % 2, h], rows).then_inc(S[f"ld_t{grp % 2}"], 16)

        blk = ctx.enter_context(nc.Block())

        @blk.sync
        def _(e):
            for a in range(2):
                e.dma_start(iobuf[0][:, a], x_dram[a]).then_inc(S["ld_x"], 16)
            load_weights(e, wst1, S["ld_up"], S["ld_hid"])
            e.wait_ge(S["hid_round"], 1)
            for h in range(H):
                for p in range(P):
                    r = D + p * HID + h * 128
                    e.dma_start(gtmp[32 * h + 4 * p:32 * h + 4 * p + 4, :],
                                d["gW1"][r:r + 128, :].rearrange("(s c) n -> s (c n)", c=DH)
                                ).then_inc(S["ld_gate"], 16)
            e.wait_ge(S["conv_round"], 1)
            e.wait_ge(S["mask_done"], 1)
            load_toep(e, 0)
            load_toep(e, 1)
            for grp in (2, 3):
                e.wait_ge(S["pe_a"], A_AT[("fir", 2, 4 * (grp - 2) + 3)] + 1)
                load_toep(e, grp)
            e.wait_ge(S["act_o"], 2 * NCH)
            load_weights(e, wstage, S["ld_w2"], S["ld_w2"])
            for t in range(NT):
                e.wait_ge(S["act_a"], A_AT[("out", 1, t)] + 1)
                e.dma_start(out_dram[t], iobuf[1][:, t]).then_inc(S["st_out"], 16)
            e.wait_ge(S["st_out"], 16 * NT)

        @blk.gpsimd
        def _(e):
            step = [0]

            def own(ins):
                step[0] += 1
                ins.then_inc(S["pool_step"], 1)
                e.wait_ge(S["pool_step"], step[0])

            own(e.memset(ident[:, :], 0.0))
            own(e.memset(mean_w[:, :], 1.0 / D))
            own(e.memset(vc("l2eps"), L2_EPS))
            own(e.memset(vc("lneps"), LN_EPS))
            own(e.memset(vc("rmseps"), RMS_EPS))
            e.affine_select(out=ident[:, :], in_=ident[:, :], compare_op=ALU.not_equal, fill=1.0,
                            base=0, pattern=[[-1, 128]], channel_multiplier=1).then_inc(S["consts"], 1)
            own(e.memset(head_w[:, :], 0.0))
            own(e.memset(gate_s[:, :], 0.0))
            own(e.memset(mtmp, 1.0))
            for q in range(4):
                own(e.memset(head_w[32 * q:32 * q + 32, 32 * q:32 * q + 32], 1.0))
            for which, op in ((0, ALU.is_gt), (1, ALU.is_ge)):
                own(e.affine_select(out=mtmp[:, which], in_=mtmp[:, which], compare_op=op, fill=0.0,
                                    base=0, pattern=[[1, 128]], channel_multiplier=-1))
            for q in range(4):
                own(e.tensor_copy(mask[32 * q:32 * q + 32], mtmp[32 * q:32 * q + 32, :, 32 * q:32 * q + 32]))
            e.memset(vec[:, 54:55], 0.0).then_inc(S["mask_done"], 1)
            e.wait_ge(S["ld_gate"], 16 * H * P)
            g = gtmp[:, :].rearrange("p (c n) -> p c n", c=DH)
            w = DH // 2
            while w:
                for h in range(H):
                    r = slice(32 * h, 32 * h + 4 * P)
                    dst = g[r, 0:w] if w > 1 else gate_s[r, :].rearrange("p (a n) -> p a n", a=1)
                    own(e.tensor_tensor(dst, g[r, 0:w], g[r, w:2 * w], ALU.add))
                w //= 2
            e.wait_ge(S["ld_vec"], 16)
            e.tensor_tensor(gate_s[:, :], gate_s[:, :], vc("share").to_broadcast([128, 2 * D]), ALU.mult
                            ).then_inc(S["gate_sum"], 1)
            part_entry(e, 2)
            own(e.memset(xnp[:, 0, :, 0:PAD].bitcast(F32), 0.0))
            own(e.memset(xnp[:, 1, :, 0:PAD].bitcast(F32), 0.0))
            own(e.memset(vpad[:, :, 0:HIST], 0.0))
            e.memset(vec[:, 54:55], 0.0).then_inc(S["pad_zero"], 1)
            e.wait_ge(S["dve_nrm"], NT)
            own(e.memset(tinv, 0.0))
            e.memset(at("tinv", 2, DH * DH)[:, :, 0:DH * DH:DH + 1], 1.0).then_inc(S["eye_done"], 1)
            e.wait_ge(S["inv_done"], 1)
            e.memset(at("block", 4096), 0.0).then_inc(S["block_zero"], 1)
            e.wait_ge(S["act_a"], A_AT[("fir", 2, 15)] + 1)
            e.memset(at("st", 2048), 0.0).then_inc(S["st_zero"], 1)
            e.wait_ge(S["ld_w2"], 16 * 5)
            e.tensor_copy(w_f[1][:, :], wstage[:, :]).then_inc(S["w2_round"], 1)

        @blk.scalar
        def _(e):
            step = [0]

            def own(ins):
                step[0] += 1
                ins.then_inc(S["act_step"], 1)

            def settle():
                e.wait_ge(S["act_step"], step[0])

            e.dma_start(vec[:, 0:NVEC], d["vec"]).then_inc(S["ld_vec"], 16)
            e.dma_start(proj, d["proj"].rearrange("p (i n) -> p i n", i=4)).then_inc(S["ld_proj"], 16)
            e.dma_start(taps, d["taps"].to_broadcast([128, 1536])).then_inc(S["ld_proj"], 16)
            e.dma_start(gx_s, d["gW1"][0:D, :]).then_inc(S["ld_proj"], 16)
            for a in range(2, NT):
                e.dma_start(iobuf[0][:, a], x_dram[a]).then_inc(S["ld_x2"], 16)
            e.dma_start(gate_2[:, :, :], d["gW2"].rearrange("(k p) n -> p k n", p=128)).then_inc(S["ld_late"], 16)
            e.dma_start(wo_w[:, :], d["Wo"]).then_inc(S["ld_late"], 16)
            e.wait_ge(S["ld_vec"], 16)
            own(e.activation(vc("atau"), vc("ltau"), ACT.Abs))
            settle()
            own(e.activation(vc("etau"), vc("atau"), ACT.Exp, scale=-1.0))
            own(e.activation(vc("eeps", 0, P), vc("epsl", 0, P), ACT.Exp, scale=-1.0))
            settle()
            e.activation(vc("lntau"), vc("etau"), ACT.Ln, bias=1.0).then_inc(S["vec_act"], 1)

            def blocks(n):
                if n >= 2:
                    e.wait_ge(S["pe_o"], 2 * (n - 1))
                for q in range(4):
                    r = slice(32 * q, 32 * q + 32)
                    e.activation(block[r, n % 2, :, :, r], alt[r, :, :, n].rearrange("p g h a t -> p (g h) a t"),
                                 ACT.Copy).then_inc(S["act_block"], 1)

            def plain_u(n, g):
                e.wait_ge(S["dve_u"], 2 * n + g + 1)
                if n:
                    e.wait_ge(S["pe_o"], 2 * (n - 1) + g + 1)
                e.activation(u_sb[:, g], ps_a[g][:, 0:128], ACT.Copy).then_inc(S["act_u"], 1)

            def output(n, g):
                e.wait_ge(S["pe_o"], 2 * n + g + 1)
                dst = o_t[:, :].rearrange("p (b t) -> p b t", b=B)[:, 4 * g:4 * g + 4, DH * n:DH * n + DH]
                e.activation(dst, ps_a[2 + g][:, 0:128].rearrange("p (b t) -> p b t", b=4), ACT.Copy
                             ).then_inc(S["act_o"], 1)

            def squares(q):
                if q >= 2:
                    e.wait_ge(S["dve_stat"], q - 1)
                p, half = STAT_ORDER[q // 2], q % 2
                e.activation(sq_p[:, half], paths[p][:, 32 * half:32 * half + 32], ACT.Square
                             ).then_inc(S["act_stat"], 1)

            for s in STEPS:
                kind, f, i = s
                a, dd = A_AT[s], D_AT[s]
                bank = ps_a[a % NRING]
                if s in ENTRY:
                    part_entry(e, ENTRY[s])
                if kind == "in":
                    e.wait_ge(S["pe_a"], a + 1)
                    e.activation(tile(x_t, i), bank[:, :], ACT.Copy).then_inc(S["act_a"], 1)
                elif kind == "mean":
                    n = NORM_AT[s]
                    if n >= 2:
                        e.wait_ge(S["dve_xn"], n - 1)
                    e.wait_ge(S["dve_d"], dd + 1)
                    e.activation(lnb[f]["sq"][:, i % 2], lnb[f]["xc"][:, i % 2], ACT.Square).then_inc(S["act_sq"], 1)
                elif kind == "var":
                    e.wait_ge(S["pe_d"], dd + 1)
                    own(e.activation(lnb[f]["y"][:, i % 2], ps_d[:, dd % NRING], ACT.Abs_reciprocal_sqrt,
                                     bias=vc("lneps")))
                    settle()
                    e.activation(lnb[f]["sq"][:, i % 2], lnb[f]["y"][:, i % 2], ACT.Square).then_inc(S["act_t"], 1)
                elif kind == "up":
                    for m in range(KT):
                        gi = KT * SET_AT[s] + m
                        e.wait_ge(S["pe_a"], a + m + 1)
                        if gi >= 4:
                            e.wait_ge(S["dve_lo"], gi - 3)
                        e.activation(gbuf[f][:, gi % 4], ps_a[(a + m) % NRING][:, :], ACT.Silu,
                                     scale=vc("s1", m)).then_inc(S["act_a"], 1)
                elif kind in ("hid1", "hid2"):
                    j = SET_AT[s]
                    set_free(e, j)
                    for m in range(KT):
                        gi = KT * j + m
                        sc = vc("g1" if kind == "hid1" else "g2", m)
                        e.wait_ge(S["pe_a"], a + m + 1)
                        e.wait_ge(S["dve_lo"], gi - 3)
                        src = ps_a[(a + m) % NRING]
                        e.activation(gbuf[f][:, gi % 4], src[:, :], ACT.Gelu, scale=sc).then_inc(S["act_step"], 1)
                        step[0] += 1
                        e.activation(acts[f][:, j % 3, 0, m], src[:, :], ACT.Gelu, scale=sc).then_inc(S["act_a"], 1)
                elif kind == "qkv":
                    k2 = i % 2
                    if i >= 2:
                        e.wait_ge(S["dve_nrm"], i - 1)
                    else:
                        e.wait_ge(S["pad_zero"], 1)
                    for w in range(4):
                        e.wait_ge(S["pe_a"], a + w + 1)
                        src = ps_a[(a + w) % NRING][:, :]
                        if w == 2:
                            e.activation(vpad[:, 2 * i:2 * i + 2, HIST:HIST + L],
                                         src.rearrange("p (b t) -> p b t", b=2), ACT.Silu).then_inc(S["act_a"], 1)
                        elif w == 3:
                            e.activation(qs[:, 4 + k2], src, ACT.Tanh, scale=0.5).then_inc(S["act_a"], 1)
                        else:
                            e.activation(qs[:, 2 * w + k2], src, ACT.Silu).then_inc(S["act_a"], 1)
                    e.wait_ge(S["act_a"], a + 2)
                    for w in range(2):
                        e.activation(qs[:, 6 + 2 * w + k2], qs[:, 2 * w + k2], ACT.Square).then_inc(S["act_ss"], 1)
                elif kind == "sumsq":
                    for w in range(2):
                        y = ny[:, 2 * w + i % 2]
                        e.wait_ge(S["pe_d"], dd + w + 1)
                        own(e.activation(y, ps_d[:, (dd + w) % NRING], ACT.Abs_reciprocal_sqrt, bias=vc("l2eps")))
                        settle()
                        e.activation(qs[:, 6 + 2 * w + i % 2], y, ACT.Square).then_inc(S["act_nt"], 1)
                elif kind in ("window", "token") and ring_of(s)[0]:
                    e.wait_ge(S["pe_a"], a + 1)
                    if kind == "window":
                        half, b = i // 8, i % 8
                        e.activation(vt[0:WIN, :, half, 4 * b:4 * b + 4].rearrange("p c w -> p w c"),
                                     bank[0:WIN, :].rearrange("p (w c) -> p w c", w=4), ACT.Copy
                                     ).then_inc(S["act_a"], 1)
                    else:
                        dst = (ktok, vtok, kbtok)[i // 4][:, 4 * (i % 4):4 * (i % 4) + 4, :]
                        e.activation(dst, bank[:, :].rearrange("p (g c) -> p g c", g=4), ACT.Copy
                                     ).then_inc(S["act_a"], 1)
                elif kind == "fir":
                    e.wait_ge(S["pe_a"], a + 1)
                    dst = pall[:, 0:3, :, 2 * i:2 * i + 2][:, :, ::-1, :].rearrange("p f t c -> p c t f")
                    e.activation(dst, bank[:, 0:384].rearrange("p (c x f) -> p c x f", c=2, x=64), ACT.Copy
                                 ).then_inc(S["act_a"], 1)
                elif kind == "chain":
                    n = i
                    if n == 0:
                        e.wait_ge(S["block_zero"], 1)
                        blocks(0)
                    plain_u(n, 0)
                    if n + 1 < NCH:
                        blocks(n + 1)
                    if n:
                        output(n - 1, 1)
                    plain_u(n, 1)
                    output(n, 0)
                    if n + 1 < NCH:
                        for g in range(2):
                            e.wait_ge(S["pe_w"], 2 * n + g + 1)
                            if n >= 2:
                                e.wait_ge(S["pe_p"], 2 * (n - 1) + g + 1)
                            e.activation(w_t[:, (n + 1) % 2, g], ps_d[:, 2 + g, 0:128], ACT.Copy, scale=-1.0
                                         ).then_inc(S["act_w"], 1)
                    else:
                        output(n, 1)
                    squares(n)
                elif kind == "stats":
                    e.wait_ge(S["path3"], 1)
                    squares(NCH)
                    squares(NCH + 1)
                    e.wait_ge(S["dve_stat"], 2 * P)
                    e.activation(st[:, :, 3:4 * P:4], st[:, :, 1:4 * P:4], ACT.Sqrt).then_inc(S["act_norm"], 1)
                elif kind == "gate":
                    if i >= 2:
                        e.wait_ge(S["pe_d"], D_AT[("logit", 2, i - 2)] + 1)
                    for m in range(2):
                        e.wait_ge(S["pe_a"], a + m + 1)
                        e.activation(hid[:, i % 2, m], ps_a[(a + m) % NRING][:, :], ACT.Gelu,
                                     bias=vc("gb1", m)).then_inc(S["act_a"], 1)
                elif kind == "mix":
                    e.wait_ge(S["dve_sub"], 1)
                    e.activation(sm[:, 64:384], sm[:, 64:384], ACT.Exp).then_inc(S["act_exp"], 1)
                    e.wait_ge(S["dve_o"], 1)
                    e.activation(mixt, o_p, ACT.Square).then_inc(S["act_osq"], 1)
                    e.wait_ge(S["dve_ms"], 1)
                    e.activation(sm[:, 896:960], sm[:, 832:896], ACT.Sqrt).then_inc(S["act_rms"], 1)
                elif kind == "out":
                    e.wait_ge(S["pe_a"], a + 1)
                    e.activation(iobuf[1][:, i], bank[:, :].rearrange("p (j c) -> p j c", j=4), ACT.Copy
                                 ).then_inc(S["act_a"], 1)

        @blk.tensor
        def _(e):
            state = dict(chain_over=False)

            def take_a(n):
                if state["chain_over"]:
                    state["chain_over"] = False
                    e.wait_ge(S["act_o"], 2 * NCH)
                    e.wait_ge(S["dve_s"], 2 * (NCH - 1))
                    e.wait_ge(S["act_w"], 2 * (NCH - 1))
                if n >= NRING:
                    e.wait_ge(S["act_a"], n - NRING + 1)
                return ps_a[n % NRING]

            def take_d(n):
                if n >= NRING:
                    e.wait_ge(S["dve_d"], n - NRING + 1)
                return ps_d[:, n % NRING]

            def start_u(n, g):
                e.wait_ge(S["act_block"], 4 * (n + 1))
                if n:
                    e.wait_ge(S["act_u"], 2 * (n - 1) + g + 1)
                for h in range(H):
                    c = slice(32 * h, 32 * h + 32)
                    last = e.matmul(ps_a[g][:, c], block[:, n % 2, 4 * g + h, 0, :], vtok[:, NCH * g + n, c],
                                    start=h == 0, stop=not n, skip_group_check=True)
                if not n:
                    last.then_inc(S["pe_p"], 1)

            def finish_u(n, g):
                e.wait_ge(S["dve_s"], 2 * (n - 1) + g + 1)
                e.wait_ge(S["act_w"], 2 * (n - 1) + g + 1)
                for b in range(4):
                    c = slice(32 * b, 32 * b + 32)
                    last = e.matmul(ps_a[g][c, 0:128], w_t[:, n % 2, g, c], s_sb[:, (n - 1) % 2, 4 * g + b, :],
                                    start=False, stop=True, skip_group_check=True)
                last.then_inc(S["pe_p"], 1)

            def next_s(n, g):
                e.wait_ge(S["dve_u"], 2 * n + g + 1)
                e.matmul(ps_d[:, g, :].rearrange("p (b c) -> p b c", b=4), ktok[:, NCH * g + n, :], u_exp[:, g],
                         start=n == 0, stop=True, skip_group_check=True).then_inc(S["pe_s"], 1)

            def output(n, g):
                e.wait_ge(S["act_u"], 2 * n + g + 1)
                if n:
                    e.wait_ge(S["act_o"], 2 * (n - 1) + g + 1)
                for h in range(H):
                    c = slice(32 * h, 32 * h + 32)
                    last = e.matmul(ps_a[2 + g][c, 0:128], u_sb[:, g, c], block[:, n % 2, 4 * g + h, 1, :],
                                    start=True, stop=not n, skip_group_check=True)
                if n:
                    for b in range(4):
                        c = slice(32 * b, 32 * b + 32)
                        last = e.matmul(ps_a[2 + g][:, c], s_sb[:, (n - 1) % 2, 4 * g + b, :],
                                        kq[:, 1, NCH * g + n, c], start=False, stop=True, skip_group_check=True)
                last.then_inc(S["pe_o"], 1)

            e.wait_ge(S["consts"], 1)
            for s in STEPS:
                kind, f, i = s
                a, dd = A_AT[s], D_AT[s]
                if kind == "in":
                    e.wait_ge(S["ld_x" if i < 2 else "ld_x2"], 32)
                    bank = take_a(a)
                    for j in range(4):
                        last = e.transpose(bank[:, 128 * j:128 * j + 128], iobuf[0][:, i, j, :], ident[:, :])
                    last.then_inc(S["pe_a"], 1)
                elif kind == "mean":
                    x_ready(e, f, i)
                    e.matmul(take_d(dd), mean_w[:, :], tile(x_t, i), start=True, stop=True).then_inc(S["pe_d"], 1)
                elif kind == "var":
                    e.wait_ge(S["act_sq"], NORM_AT[("mean", f, i)] + 1)
                    e.matmul(take_d(dd), mean_w[:, :], lnb[f]["sq"][:, i % 2], start=True, stop=True
                             ).then_inc(S["pe_d"], 1)
                elif kind == "up":
                    if i == 0:
                        e.wait_ge(S["up_round" if f == 0 else "w2_round"], 1)
                    e.wait_ge(S["dve_xn"], VAR_AT[("var", f, i)] + 1)
                    for m in range(KT):
                        for bank, o, done in ((take_a(a + m)[:, :], 0, "pe_a"), (take_d(dd + m), 512, "pe_d")):
                            for part in range(2):
                                last = e.matmul(bank, w_f[f][:, o + 128 * m:o + 128 * m + 128],
                                                xn_f[f][:, i % 2, part], start=part == 0, stop=part == 1)
                            last.then_inc(S[done], 1)
                elif kind in ("hid1", "hid2"):
                    if kind == "hid1" and i == 0 and f == 0:
                        e.wait_ge(S["hid_round"], 1)
                    c = USED_AT[s]
                    o = 1024 if kind == "hid1" else 3072
                    for m in range(KT):
                        bank = take_a(a + m)
                        for k in range(KT):
                            if m == 0:
                                e.wait_ge(S["dve_lo"], KT * c + k + 1)
                            for part in range(2):
                                last = e.matmul(bank[:, :], w_f[f][:, o + 512 * k + 128 * m:o + 512 * k + 128 * m + 128],
                                                acts[f][:, c % 3, part, k], start=k == 0 and part == 0,
                                                stop=k == KT - 1 and part == 1)
                        last.then_inc(S["pe_a"], 1)
                elif kind == "down":
                    c = USED_AT[s]
                    bank = take_d(dd)
                    for k in range(KT):
                        e.wait_ge(S["dve_lo"], KT * c + k + 1)
                        for part in range(2):
                            last = e.matmul(bank, w_f[f][:, 5120 + 128 * k:5120 + 128 * k + 128],
                                            acts[f][:, c % 3, part, k], start=k == 0 and part == 0,
                                            stop=k == KT - 1 and part == 1)
                    last.then_inc(S["pe_d"], 1)
                elif kind == "qkv":
                    if i == 0:
                        e.wait_ge(S["pad_zero"], 1)
                    e.wait_ge(S["dve_xn"], VAR_AT[("var", 2, i)] + 1)
                    for w in range(4):
                        bank = take_a(a + w)[:, :].rearrange("p (b t) -> p b t", b=2)
                        todo = [(w * TAPS + j, 1 + j) for j in range(TAPS)] if w < 3 else [(12, PAD)]
                        todo = [(ww, o, hw, hx) for ww, o in todo for hw, hx in ((0, 0), (0, 1), (1, 0))]
                        for n, (ww, o, hw, hx) in enumerate(todo):
                            last = e.matmul(bank, conv_w[:, hw, ww], xnp[:, hx, 2 * i:2 * i + 2, o:o + L],
                                            start=n == 0, stop=n == len(todo) - 1)
                        last.then_inc(S["pe_a"], 1)
                elif kind == "sumsq":
                    for w in range(2):
                        e.wait_ge(S["act_ss"], 2 * i + w + 1)
                        e.matmul(take_d(dd + w), head_w[:, :], qs[:, 6 + 2 * w + i % 2], start=True, stop=True
                                 ).then_inc(S["pe_d"], 1)
                elif kind in ("window", "token"):
                    if i == 0:
                        e.wait_ge(S["dve_nrm"], NT)
                    on_a = ring_of(s)[0]
                    bank = take_a(a) if on_a else take_d(dd)
                    for w in range(4):
                        if kind == "window":
                            o = DH * (2 * w + i // 8)
                            last = e.transpose(bank[0:WIN, 128 * w:128 * w + 128], vpad[:, i % 8, o:o + WIN], ident[:, :])
                        else:
                            src = (kn, vb, kq[:, 0])[i // 4][:, 4 * (i % 4) + w, :]
                            last = e.transpose(bank[:, 128 * w:128 * w + 128], src, ident[:, :])
                    last.then_inc(S["pe_a" if on_a else "pe_d"], 1)
                elif kind == "gram":
                    for h in range(H):
                        bank = take_d(dd + h)
                        r = slice(32 * h, 32 * h + 32)
                        for n in range(NCH):
                            for b in range(4):
                                c = slice(32 * b, 32 * b + 32)
                                last = e.matmul(bank[c, 64 * n:64 * n + 64].rearrange("p (a t) -> p a t", a=2),
                                                kn[r, NCH * i + n, c], kq[r, :, NCH * i + n, c],
                                                start=True, stop=True)
                        last.then_inc(S["pe_d"], 1)
                elif kind == "fir":
                    grp = i // 4
                    if i == 0:
                        e.wait_ge(S["act_a"], A_AT[("token", 2, 11)])
                        e.wait_ge(S["dve_d"], D_AT[("gram", 2, 0)])
                    if i % 4 == 0:
                        e.wait_ge(S[f"ld_t{grp % 2}"], 64 * (grp // 2 + 1))
                    bank = take_a(a)
                    for c2 in range(2):
                        for half in range(2):
                            for h in range(H):
                                dl = (2 * i + c2) % 8
                                o = 192 * c2 + WIN * (1 - half)
                                last = e.matmul(bank[32 * h:32 * h + 32, o:o + WIN],
                                                vt[0:WIN, DH * h + 2 * i + c2, half, :], toep[0:WIN, grp % 2, h, dl],
                                                start=True, stop=True)
                    last.then_inc(S["pe_a"], 1)
                elif kind == "chain":
                    n = i
                    if n == 0:
                        e.wait_ge(S["act_a"], a)
                        e.wait_ge(S["dve_d"], dd)
                        start_u(0, 0)
                        start_u(0, 1)
                    else:
                        finish_u(n, 0)
                        output(n - 1, 1)
                    if n < NCH - 1:
                        next_s(n, 0)
                    if n:
                        finish_u(n, 1)
                    output(n, 0)
                    if n < NCH - 1:
                        next_s(n, 1)
                        for g in range(2):
                            e.wait_ge(S["act_block"], 4 * (n + 2))
                            if n:
                                e.wait_ge(S["act_w"], 2 * (n - 1) + g + 1)
                            for h in range(H):
                                c = slice(32 * h, 32 * h + 32)
                                last = e.matmul(ps_d[c, 2 + g, 0:128], kbtok[:, NCH * g + n + 1, c],
                                                block[:, (n + 1) % 2, 4 * g + h, 0, :], start=True, stop=True)
                            last.then_inc(S["pe_w"], 1)
                        start_u(n + 1, 0)
                        start_u(n + 1, 1)
                    else:
                        output(n, 1)
                    state["chain_over"] = n == NCH - 1
                elif kind == "gate":
                    if i == 0:
                        e.wait_ge(S["st_turned"], 1)
                    for m in range(2):
                        c = slice(128 * m, 128 * m + 128)
                        bank = take_a(a + m)[:, :]
                        for n, (hw, hx) in enumerate(((0, 0), (0, 1), (1, 0))):
                            e.matmul(bank.rearrange("p (b t) -> p b t", b=2), gate_x[:, hw, c],
                                     xnp[:, hx, 2 * i:2 * i + 2, PAD:PAD + L], start=n == 0, stop=False)
                        e.matmul(bank, gate_s[:, c], tile(st_t, i), start=False, stop=True).then_inc(S["pe_a"], 1)
                elif kind == "logit":
                    bank = take_d(dd)
                    if i == 0:
                        e.wait_ge(S["ld_late"], 32)
                    for m in range(2):
                        e.wait_ge(S["act_a"], A_AT[("gate", 2, i)] + m + 1)
                        last = e.matmul(bank, gate_2[:, m, :], hid[:, i % 2, m], start=m == 0, stop=m == 1)
                    last.then_inc(S["pe_d"], 1)
                elif kind == "wo":
                    if i == 0:
                        e.wait_ge(S["o_turned"], 1)
                    e.matmul(take_d(dd), wo_w[:, :], tile(o_c, i), start=True, stop=True).then_inc(S["pe_d"], 1)
                elif kind == "out":
                    e.wait_ge(S["dve_d"], D_AT[("down", 1, i)] + 1)
                    bank = take_a(a)
                    for j in range(4):
                        last = e.transpose(bank[:, 128 * j:128 * j + 128], x_t[:, i * TILE + 128 * j:i * TILE + 128 * j + 128],
                                           ident[:, :])
                    last.then_inc(S["pe_a"], 1)

        @blk.vector
        def _(e):
            step = [0]

            def own(ins):
                step[0] += 1
                ins.then_inc(S["dve_step"], 1)

            def settle():
                e.wait_ge(S["dve_step"], step[0])

            def numbers():
                e.wait_ge(S["vec_act"], 1)
                own(e.tensor_scalar(vc("s3h"), vc("s3"), 0.5, None, ALU.mult))
                own(e.tensor_scalar(vc("mtau"), vc("ltau"), 0.0, 0.5, ALU.max, ALU.add))
                own(e.tensor_scalar(vc("epsd", 0, P), vc("eeps", 0, P), 1.0, 5.0, ALU.add, ALU.mult))
                settle()
                own(e.tensor_tensor(vc("mtau"), vc("mtau"), vc("lntau"), ALU.add))
                own(e.reciprocal(vc("eps", 0, P), vc("epsd", 0, P)))
                settle()
                own(e.reciprocal(vc("itau"), vc("mtau")))
                own(e.tensor_reduce(vc("rest"), vc("eps", 0, P), AX_X, ALU.add))
                settle()
                own(e.tensor_scalar(vc("rest"), vc("rest"), -1.0, 1.0, ALU.mult, ALU.add))

            def projections():
                e.wait_ge(S["ld_proj"], 48)
                for w in range(3):
                    own(e.tensor_tensor(conv_s[:, TAPS * w:TAPS * w + TAPS],
                                        taps[:, 512 * w:512 * w + 512].rearrange("p (j n) -> p j n", j=TAPS),
                                        proj[:, w:w + 1, :].to_broadcast([128, TAPS, 128]), ALU.mult))
                own(e.tensor_copy(conv_s[:, 12], proj[:, 3]))
                own(e.tensor_copy(gate_x[:, 0], gx_s))
                settle()
                own(e.tensor_copy(conv_w[:, 0], conv_s))
                own(e.tensor_tensor(gate_x[:, 1], gx_s, gate_x[:, 0].bitcast(F32), ALU.subtract))
                settle()
                e.tensor_tensor(conv_w[:, 1], conv_s, conv_w[:, 0].bitcast(F32), ALU.subtract
                                ).then_inc(S["conv_round"], 1)
                e.wait_ge(S["ld_late"], 32)
                own(e.tensor_scalar(wo_w[:, :], wo_w[:, :], vc("norm"), None, ALU.mult))

            def refine(bank, t, y, src, eps, free):
                e.scalar_tensor_tensor(out=t, in0=bank, scalar=eps, in1=t, op0=ALU.add, op1=ALU.mult
                                       ).then_inc(S["dve_d"], 1)
                own(e.tensor_tensor(src, src, y, ALU.mult))
                free()
                own(e.tensor_scalar(t, t, -0.5, 1.5, ALU.mult, ALU.add))
                settle()

            def spread_u(n, g):
                e.wait_ge(S["pe_p"], 2 * n + g + 1)
                e.tensor_tensor(u_exp[:, g], ps_a[g][:, 0:128].unsqueeze(1).to_broadcast([128, 4, 128]),
                                head_w[:, 0:128:32].unsqueeze(2).to_broadcast([128, 4, 128]), ALU.mult
                                ).then_inc(S["dve_u"], 1)

            def mask_s(n, g):
                e.wait_ge(S["pe_s"], 2 * n + g + 1)
                if n:
                    e.wait_ge(S["pe_o"], 2 * (n - 1) + g + 1)
                e.tensor_tensor(s_sb[:, n % 2, 4 * g:4 * g + 4, :], ps_d[:, g, :].rearrange("p (b c) -> p b c", b=4),
                                head_w[:, :].unsqueeze(1).to_broadcast([128, 4, 128]), ALU.mult
                                ).then_inc(S["dve_s"], 1)

            def sums(q):
                p, r = STAT_ORDER[q // 2], slice(32 * (q % 2), 32 * (q % 2) + 32)
                own(e.tensor_reduce(st[:, r, 4 * p], paths[p][:, r], AX_X, ALU.add))

            def absolute_sums(q):
                p, r = STAT_ORDER[q // 2], slice(32 * (q % 2), 32 * (q % 2) + 32)
                own(e.tensor_reduce(st[:, r, 4 * p + 2], paths[p][:, r], AX_X, ALU.add, apply_absolute_value=True))

            def square_sums(q):
                p, r = STAT_ORDER[q // 2], slice(32 * (q % 2), 32 * (q % 2) + 32)
                e.wait_ge(S["act_stat"], q + 1)
                e.tensor_reduce(st[:, r, 4 * p + 1], sq_p[:, q % 2], AX_X, ALU.add).then_inc(S["dve_stat"], 1)

            for s in STEPS:
                kind, f, i = s
                a, dd = A_AT[s], D_AT[s]
                if s in ENTRY:
                    part_entry(e, ENTRY[s])
                if kind == "mean":
                    e.wait_ge(S["pe_d"], dd + 1)
                    x_ready(e, f, i)
                    if NORM_AT[s] >= 2:
                        e.wait_ge(S["act_t"], NORM_AT[s] - 1)
                    e.tensor_tensor(lnb[f]["xc"][:, i % 2], tile(x_t, i), ps_d[:, dd % NRING], ALU.subtract
                                    ).then_inc(S["dve_d"], 1)
                elif kind == "var":
                    b = {k: v[:, i % 2] for k, v in lnb[f].items()}
                    e.wait_ge(S["act_t"], VAR_AT[s] + 1)
                    refine(ps_d[:, dd % NRING], b["sq"], b["y"], b["xc"], LN_EPS,
                           lambda: e.wait_ge(S["dve_d"], dd + 1))
                    own(e.tensor_tensor(b["u"], b["xc"], b["sq"], ALU.mult))
                    settle()
                    if f == 2:
                        hi, lo = (xnp[:, part, 2 * i:2 * i + 2, PAD:PAD + L] for part in range(2))
                        u = b["u"].rearrange("p (b t) -> p b t", b=2)
                    else:
                        if i >= 2:
                            e.wait_ge(S["pe_d"], D_AT[("up", f, i - 2)] + KT)
                        hi, lo, u = xn_f[f][:, i % 2, 0], xn_f[f][:, i % 2, 1], b["u"]
                    own(e.tensor_copy(hi, u))
                    settle()
                    e.tensor_tensor(lo, u, hi.bitcast(F32), ALU.subtract).then_inc(S["dve_xn"], 1)
                    if s == ("var", 0, 0):
                        e.wait_ge(S["ld_up"], 32)
                        e.tensor_copy(w_f[0][:, 0:1024], wst1[:, 0:1024]).then_inc(S["up_round"], 1)
                elif kind == "up":
                    j = SET_AT[s]
                    set_free(e, j)
                    for m in range(KT):
                        e.wait_ge(S["pe_d"], dd + m + 1)
                        e.wait_ge(S["act_a"], a + m + 1)
                        e.scalar_tensor_tensor(out=hbuf[f][:, m % 2], in0=ps_d[:, (dd + m) % NRING], scalar=vc("s2", m),
                                               in1=gbuf[f][:, (KT * j + m) % 4], op0=ALU.mult, op1=ALU.mult
                                               ).then_inc(S["dve_d"], 1)
                        e.wait_ge(S["dve_d"], dd + m + 1)
                        own(e.tensor_copy(acts[f][:, j % 3, 0, m], hbuf[f][:, m % 2]))
                        settle()
                        e.tensor_tensor(acts[f][:, j % 3, 1, m], hbuf[f][:, m % 2],
                                        acts[f][:, j % 3, 0, m].bitcast(F32), ALU.subtract).then_inc(S["dve_lo"], 1)
                    if s == ("up", 0, 0):
                        e.wait_ge(S["ld_hid"], 48)
                        e.tensor_copy(w_f[0][:, 1024:5632], wst1[:, 1024:5632]).then_inc(S["hid_round"], 1)
                    if s == ("up", 0, 1):
                        numbers()
                elif kind in ("hid1", "hid2"):
                    j = SET_AT[s]
                    for m in range(KT):
                        e.wait_ge(S["act_a"], a + m + 1)
                        e.tensor_tensor(acts[f][:, j % 3, 1, m], gbuf[f][:, (KT * j + m) % 4],
                                        acts[f][:, j % 3, 0, m].bitcast(F32), ALU.subtract).then_inc(S["dve_lo"], 1)
                    if s == ("hid1", 0, 1):
                        projections()
                elif kind == "down":
                    e.wait_ge(S["pe_d"], dd + 1)
                    e.scalar_tensor_tensor(out=tile(x_t, i), in0=ps_d[:, dd % NRING], scalar=vc("s3h"), in1=tile(x_t, i),
                                           op0=ALU.mult, op1=ALU.add).then_inc(S["dve_d"], 1)
                elif kind == "sumsq":
                    k2 = i % 2
                    e.wait_ge(S["act_a"], A_AT[("qkv", 2, i)] + 4)
                    own(e.tensor_scalar(qs[:, 4 + k2], qs[:, 4 + k2], 0.5, 0.5, ALU.mult, ALU.add))
                    settle()
                    beta = qs[:, 4 + k2].rearrange("p (b t) -> p b t", b=2)
                    own(e.tensor_tensor(chunked(vb, i),
                                        vpad[:, 2 * i:2 * i + 2, HIST:HIST + L].rearrange("p b (n t) -> p b n t", n=NCH),
                                        plain(qs[:, 4 + k2]), ALU.mult))
                    for w in range(2):
                        src, t, y = qs[:, 2 * w + k2], qs[:, 6 + 2 * w + k2], ny[:, 2 * w + k2]
                        e.wait_ge(S["act_nt"], 2 * i + w + 1)
                        refine(ps_d[:, (dd + w) % NRING], t, y, src, L2_EPS,
                               lambda: e.wait_ge(S["dve_d"], dd + w + 1))
                        own(e.tensor_tensor(chunked(kq[:, 1] if w == 0 else kn, i), plain(src), plain(t), ALU.mult))
                    settle()
                    e.tensor_tensor(chunked(kq[:, 0], i), chunked(kn, i), plain(qs[:, 4 + k2]), ALU.mult
                                    ).then_inc(S["dve_nrm"], 1)
                elif kind == "vpath":
                    e.wait_ge(S["dve_nrm"], NT)
                    own(e.transpose(paths[4].rearrange("p t c -> p (t c)"),
                                    vpad[:, :, HIST:HIST + L].rearrange("p b (w t) -> p t b w", t=64)))
                elif kind in ("window", "token") and ring_of(s)[1]:
                    e.wait_ge(S["pe_d"], dd + 1)
                    bank = ps_d[:, dd % NRING]
                    if kind == "window":
                        half, b = i // 8, i % 8
                        e.tensor_copy(vt[0:WIN, :, half, 4 * b:4 * b + 4].rearrange("p c w -> p w c"),
                                      bank[0:WIN, :].rearrange("p (w c) -> p w c", w=4)).then_inc(S["dve_d"], 1)
                    else:
                        dst = (ktok, vtok, kbtok)[i // 4][:, 4 * (i % 4):4 * (i % 4) + 4, :]
                        e.tensor_copy(dst, bank.rearrange("p (g c) -> p g c", g=4)).then_inc(S["dve_d"], 1)
                elif kind == "gram":
                    if i == 0:
                        settle()
                    mk = mask[:, :, :].rearrange("p a t -> p (a t)").unsqueeze(1).to_broadcast([128, NCH, 64])
                    for h in range(H):
                        e.wait_ge(S["pe_d"], dd + h + 1)
                        e.tensor_tensor(alt[:, i, h].rearrange("p n a t -> p n (a t)"),
                                        ps_d[:, (dd + h) % NRING].rearrange("p (n x) -> p n x", n=NCH), mk, ALU.mult
                                        ).then_inc(S["dve_d"], 1)
                elif kind == "inverse":
                    e.wait_ge(S["dve_d"], dd)
                    e.wait_ge(S["eye_done"], 1)
                    at_a = alt[:, :, :, :, 0, :].rearrange("p g h n t -> p g t (h n)")
                    own(e.transpose(lmat.rearrange("p g i j -> p (g i j)"), at_a))
                    settle()
                    for j in range(DH - 1):
                        k = DH - 1 - j
                        sub = tinv[:, :, j + 1:DH, 0:j + 1]
                        prod = tmp[:, 0:2 * k * (j + 1)].rearrange("p (g i c) -> p g i c", g=2, i=k)
                        own(e.tensor_tensor(prod, lmat[:, :, j + 1:DH, j:j + 1].to_broadcast([128, 2, k, j + 1]),
                                            tinv[:, :, j:j + 1, 0:j + 1].to_broadcast([128, 2, k, j + 1]), ALU.mult))
                        settle()
                        own(e.tensor_tensor(sub, sub, prod, ALU.subtract))
                        settle()
                    e.transpose(at_a, tinv.rearrange("p g i j -> p (g i j)")).then_inc(S["inv_done"], 1)
                elif kind == "chain":
                    n = i
                    spread_u(n, 0)
                    if n < NCH - 1:
                        mask_s(n, 0)
                    spread_u(n, 1)
                    if n == 0:
                        e.wait_ge(S["st_zero"], 1)
                    sums(n)
                    if n < NCH - 1:
                        mask_s(n, 1)
                    absolute_sums(n)
                    square_sums(n)
                elif kind == "stats":
                    e.wait_ge(S["act_o"], 2 * NCH)
                    e.transpose(paths[3].rearrange("p t c -> p (t c)"),
                                o_t[:, :].rearrange("p (x t) -> p t x", t=64)).then_inc(S["path3"], 1)
                    e.wait_ge(S["path3"], 1)
                    for q in (NCH, NCH + 1):
                        sums(q)
                        absolute_sums(q)
                        square_sums(q)
                    e.wait_ge(S["act_norm"], 1)
                    e.wait_ge(S["dve_step"], step[0])
                    e.transpose(st_t[:, :].rearrange("p (x t) -> p t x", t=64),
                                st.rearrange("p t c -> p (t c)")).then_inc(S["st_turned"], 1)
                elif kind == "logit":
                    e.wait_ge(S["pe_d"], dd + 1)
                    e.tensor_scalar(tile(lg, i), ps_d[:, dd % NRING], vc("gb2"), vc("itau"), ALU.add, ALU.mult
                                    ).then_inc(S["dve_d"], 1)
                elif kind == "mix":
                    e.wait_ge(S["dve_d"], dd)
                    own(e.transpose(pl.rearrange("p t c -> p (t c)"), lg[:, :].rearrange("p (x t) -> p t x", t=64)))
                    settle()
                    lo5 = pl[:, :, 0:P]
                    mx, ex, su, pr, ms = (sm[:, 0:64], sm[:, 64:384], sm[:, 384:448], sm[:, 448:768], sm[:, 768:832])
                    ex5 = ex.rearrange("p (t c) -> p t c", c=P)
                    pr5 = pr.rearrange("p (t c) -> p t c", c=P)

                    def per_token(v):
                        return v.unsqueeze(2).to_broadcast([128, 64, P])

                    own(e.tensor_reduce(mx, lo5, AX_X, ALU.max))
                    settle()
                    e.tensor_tensor(ex5, lo5, per_token(mx), ALU.subtract).then_inc(S["dve_sub"], 1)
                    e.wait_ge(S["act_exp"], 1)
                    own(e.tensor_reduce(su, ex5, AX_X, ALU.add))
                    settle()
                    own(e.reciprocal(su, su))
                    settle()
                    own(e.tensor_tensor(pr5, ex5, per_token(su), ALU.mult))
                    settle()
                    own(e.scalar_tensor_tensor(out=pr5, in0=pr5, scalar=vc("rest"),
                                               in1=vc("eps", 0, P).unsqueeze(1).to_broadcast([128, 64, P]),
                                               op0=ALU.mult, op1=ALU.add))
                    settle()
                    for p in range(P):
                        w = pr5[:, :, p:p + 1].to_broadcast([128, 64, DH])
                        own(e.tensor_tensor(mixt if p else o_p, paths[p], w, ALU.mult))
                        settle()
                        if p:
                            add = e.tensor_tensor(o_p, o_p, mixt, ALU.add)
                            if p < P - 1:
                                own(add)
                                settle()
                            else:
                                add.then_inc(S["dve_o"], 1)
                    e.wait_ge(S["act_osq"], 1)
                    own(e.tensor_reduce(ms, mixt, AX_X, ALU.add))
                    settle()
                    var, rt, t2 = sm[:, 832:896], sm[:, 896:960], sm[:, 960:1024]
                    e.tensor_scalar(var, ms, 1.0 / DH, RMS_EPS, ALU.mult, ALU.add).then_inc(S["dve_ms"], 1)
                    e.wait_ge(S["act_rms"], 1)
                    own(e.reciprocal(rt, rt))
                    settle()
                    own(e.tensor_tensor(t2, rt, rt, ALU.mult))
                    settle()
                    own(e.tensor_tensor(t2, t2, var, ALU.mult))
                    settle()
                    own(e.tensor_scalar(t2, t2, -0.5, 1.5, ALU.mult, ALU.add))
                    settle()
                    own(e.tensor_tensor(rt, rt, t2, ALU.mult))
                    settle()
                    own(e.tensor_tensor(o_p, o_p, rt.unsqueeze(2).to_broadcast([128, 64, DH]), ALU.mult))
                    settle()
                    e.transpose(o_c[:, :].rearrange("p (x t) -> p t x", t=64), o_p.rearrange("p t c -> p (t c)")
                                ).then_inc(S["o_turned"], 1)
                elif kind == "wo":
                    e.wait_ge(S["pe_d"], dd + 1)
                    e.tensor_tensor(tile(x_t, i), tile(x_t, i), ps_d[:, dd % NRING], ALU.add).then_inc(S["dve_d"], 1)


_OUT = (B * L, D)


def lay_out(x):
    import numpy as np

    def cols(name):
        return np.asarray(x[name]).reshape(-1, 128).T

    a = {k: np.asarray(v) for k, v in x.items()}
    fir = np.zeros((D, 128, 3), np.float32)
    for n, k in enumerate(("fir_s", "fir_m", "fir_l")):
        w = a["L0_attn_" + k]
        fir[:, WIN - w.shape[1]:WIN, n] = w
    gw2 = np.zeros((2 * D, H, 32), np.float32)
    gw2[:, :, :P] = a["L0_attn_gW2"].reshape(2 * D, H, P)
    gb2 = np.zeros((H, 32), np.float32)
    gb2[:, :P] = a["L0_attn_gb2"].reshape(H, P)
    vec = [cols("L0_ffn_w1_s"), cols("L0_ffn_w2_s"), cols("L0_ffn_h1_s"), cols("L0_ffn_h2_s"), cols("L0_ffn_w3_s"),
           np.tile(a["L0_attn_norm_w"], H)[:, None], np.repeat(a["L0_attn_log_tau"], DH)[:, None],
           gb2.reshape(128, 1), cols("L0_attn_gb1"), np.repeat(a["L0_attn_eps_logit"], DH, axis=0),
           np.tile(np.array([1 / DH, 1 / DH, 1 / DH, 1], np.float32), 32)[:, None]]
    taps = np.stack([a["L0_attn_conv_" + k].T for k in "qkv"]).reshape(1, 3 * TAPS * D)
    proj = [a["L0_attn_Wq"], a["L0_attn_Wk"], a["L0_attn_Wv"], np.repeat(a["L0_attn_Wb"], DH, axis=1)]
    out = {
        "x": a["L0_attn_hidden_states"].reshape(B * L, D),
        "w1": a["L0_ffn_w1_w"].T, "w2": a["L0_ffn_w2_w"].T, "h1": a["L0_ffn_h1_w"].T, "h2": a["L0_ffn_h2_w"].T,
        "w3": a["L0_ffn_w3_w"].T, "vec": np.concatenate(vec, axis=1), "proj": np.concatenate(proj, axis=1),
        "taps": taps, "fir": fir.reshape(D, 384), "gW1": a["L0_attn_gW1"], "gW2": gw2.reshape(2 * D, 128),
        "Wo": a["L0_attn_Wo"],
    }
    return {k: np.ascontiguousarray(v) for k, v in out.items()}


def kernel(**inputs):
    import concourse.bacc as bacc
    from concourse.bass_utils import run_bass_kernel_spmd

    nc = bacc.Bacc("TRN2", target_bir_lowering=False, num_devices=1)
    arrays = lay_out(inputs)
    d = {k: nc.dram_tensor("in_" + k, v.shape, mybir.dt.from_np(v.dtype), kind="ExternalInput").ap() for k, v in arrays.items()}
    out = nc.dram_tensor("y", _OUT, F32, kind="ExternalOutput").ap()
    program(nc, d, out)
    r = run_bass_kernel_spmd(nc, [{"in_" + k: v for k, v in arrays.items()}], core_ids=[0])
    return r.results[0]["y"].reshape(B, L, D)
```

```python
from contextlib import ExitStack

import concourse.bass as bass
from concourse import mybir

ALU = mybir.AluOpType
ACT = mybir.ActivationFunctionType
AX_X = mybir.AxisListType.X
F32 = mybir.dt.float32
F32R = mybir.dt.float32r

B, L, D, H, P = 8, 256, 128, 4, 5
DH = D // H
HID = 512
KT = HID // 128
TILE = 512
NT = B * L // TILE
NCH = L // DH
TAPS = 4
PAD = 4
HIST, WIN = 64, 96
LN_EPS, L2_EPS, RMS_EPS = 1e-5, 1e-6, 1e-5
MIX_SPLIT = 24
NRING = 4

def ffn_steps(f):
    last = f == 1
    s = [] if last else [("in", f, 0), ("in", f, 1)]
    s += [("mean", f, 0), ("mean", f, 1)]
    s += [("var", f, 0), ("var", f, 1)]
    for a in range(0, NT, 2):
        b = a + 1
        more = a + 2 < NT
        s += [("up", f, a), ("up", f, b)]
        if more and last:
            s += [("hid1", f, a), ("scale", 2, 1), ("hid1", f, b), ("wo", 2, 2), ("wo", 2, 3), ("hid2", f, a),
                  ("mean", f, 2), ("mean", f, 3), ("var", f, 2), ("var", f, 3), ("hid2", f, b)]
        elif more:
            s += [("hid1", f, a), ("in", f, a + 2), ("in", f, b + 2), ("mean", f, a + 2), ("mean", f, b + 2),
                  ("flag", f, 0), ("flag", f, 1), ("hid1", f, b), ("var", f, a + 2), ("hid2", f, a),
                  ("var", f, b + 2), ("hid2", f, b)]
        elif last:
            s += [("hid1", f, a), ("hid1", f, b), ("hid2", f, a), ("hid2", f, b)]
        else:
            s += [("hid1", f, a), ("mean", 2, 0), ("mean", 2, 1), ("gsum", f, 1), ("hid1", f, b),
                  ("var", 2, 0), ("var", 2, 1), ("hid2", f, a), ("hid2", f, b)]
        s += [("down", f, a), ("down", f, b)]
        s += [("gsum", f, 0)] if more and not last else []
        s += [("out", f, a), ("out", f, b)] if last else []
    return s


def att_steps():
    s = []
    for t in range(NT):
        s.append(("qkv", 2, t))
        if t + 2 < NT:
            s += [("mean", 2, t + 2), ("var", 2, t + 2)]
        if t:
            s.append(("sumsq", 2, t - 1))
    s += [("sumsq", 2, NT - 1), ("gram", 2, 0), ("inverse", 2, 0)]
    s += [("window", 2, i) for i in range(16)]
    s += [("gram", 2, 1), ("inverse", 2, 1)]
    s += [("token", 2, i) for i in range(12)]
    s += [("fir", 2, i) for i in range(16)]
    s += [("chain", 2, n) for n in range(NCH)]
    s += [("stats", 2, 0)]
    for half in range(2):
        s += [("gate", 2, 2 * half + i) for i in range(2)] + [("logit", 2, 2 * half + i) for i in range(2)]
        s += [("soft", 2, 0), ("mix", 2, 0)] if half == 0 else []
    s += [("scale", 2, 0), ("soft", 2, 1), ("wo", 2, 0), ("wo", 2, 1)]
    return s


STEPS = ffn_steps(0) + att_steps() + ffn_steps(1)

RING_A = {"in": 1, "gsum": 1, "up": KT, "hid1": KT, "hid2": KT, "out": 1, "qkv": 4, "window": 1, "token": 1, "fir": 1,
          "gate": 2}
RING_D = {"mean": 1, "flag": 1, "var": 1, "up": KT, "down": 1, "sumsq": 2, "gram": H, "logit": 1, "wo": 1}


def ring_of(step):
    kind, _, i = step
    return RING_A.get(kind, 0), RING_D.get(kind, 0)


def before(kinds, weight=lambda s: 1):
    out, n = {}, 0
    for s in STEPS:
        out[s] = n
        if s[0] in kinds:
            n += weight(s)
    return out, n


ANY = {s[0] for s in STEPS}
A_AT, _ = before(ANY, lambda s: ring_of(s)[0])
D_AT, _ = before(ANY, lambda s: ring_of(s)[1])
LAYERS = ("up", "hid1", "hid2")
SET_AT, _ = before(LAYERS)
USED_AT, _ = before(("hid1", "hid2", "down"))
USERS = [s for s in STEPS if s[0] in ("hid1", "hid2", "down")]
NORM_AT, _ = before(("mean",))
VAR_AT, _ = before(("var",))
UP_AT, _ = before(("up",))

STAT_ORDER = (0, 1, 2, 4, 3)

V = dict(s1=0, s2=4, g1=8, g2=12, s3=16, norm=17, ltau=18, gb2=19, gb1=20, epsl=22,
         atau=28, etau=29, eeps=30, lntau=35, s3h=36, itau=37, eps=38, rest=43, l2eps=44, lneps=45, rmseps=46,
         mtau=47, epsd=48)
NVEC = 27

ARENA = 38912
AO = dict(tinv=0, lmat=2048, tmp=4096, vt=5632, ny=34304, kq=13824, ktok=17920, vtok=19968,
          alt=22016, paths=26112, kn=26112, vb=28160, ln=30208, kbtok=32256, vpad=36352,
          uexp=0, wt=1024, ssb=1536, sq=3584, st=5632, ot=7680, block=9728,
          stt=0, hid=2048, lg=4096, pl=6144, small=12288, o=36352, oc=37376)


def program(nc, d, out):
    ctx = ExitStack()
    with ctx:
        def sb(name, shape, dt=F32, c=ctx):
            return c.enter_context(nc.sbuf_tensor(name, shape, dt))

        def sem(name):
            return ctx.enter_context(nc.semaphore(name))

        ps_a = [ctx.enter_context(nc.psum_tensor(f"ps_a{i}", [128, 512], F32)) for i in range(NRING)]
        ps_d = ctx.enter_context(nc.psum_tensor("ps_d", [128, NRING, 512], F32))

        x_t = sb("x_t", [128, B * L])
        ident = sb("ident", [128, 128])
        mean_w = sb("mean_w", [128, 128])
        head_w = sb("head_w", [128, 128])
        mask = sb("mask", [128, 2, DH])
        gate_x = sb("gate_x", [128, 2, 2 * D], F32R)
        gate_s = sb("gate_s", [128, 2 * D])
        gate_2 = sb("gate_2", [128, 2, 128])
        wo_w = sb("wo_w", [128, D])
        low_max = sb("low_max", [128, 3])
        low_any = sb("low_any", [128, 2], mybir.dt.int32)
        pick = sb("pick", [128, 48])
        vec = sb("vec", [128, 56])
        ct = ExitStack()
        toep = sb("toep", [128, 2, H, WIN, 8], F32, ct)
        ct.close()
        cs = ExitStack()
        wstage = sb("wstage1", [128, 5632], F32, cs)
        cs.close()
        xn_1 = sb("xn1", [128, 2, 2, TILE], F32R)
        gbuf_1 = sb("gbuf1", [128, 4, TILE])
        iobuf_1 = sb("iobuf1", [128, 4, 4, 128])

        c1 = ExitStack()
        w_f = [sb("w_f0", [128, 5632], F32R, c1)]
        conv_w = sb("conv_w", [128, 2, 13, 128], F32R, c1)
        acts = [sb("acts0", [128, 3, 2, KT, TILE], F32R, c1)]
        ghbuf = sb("ghbuf0", [128, 6, TILE], F32, c1)
        cs = ExitStack()
        wst1 = sb("wstage0", [128, 5632], F32, cs)
        cs.close()
        wlow = [sb("w_low0", [128, 5632], F32R, c1)]
        sb("gap0", [128, AO["ln"] - 29952], F32, c1)
        ln_0 = sb("ln0", [128, 8, TILE], F32, c1)
        g_rows = sb("g_rows", [128, 2, P, 2 * D], F32, c1)
        sb("gap1", [128, ARENA - 36864], F32, c1)
        iobuf_0 = sb("iobuf0", [128, 4, 4, 128], F32, c1)
        xn_f = [sb("xn0", [128, 2, 2, TILE], F32R, c1)]
        c1.close()
        c2 = ExitStack()
        arena = sb("arena", [128, ARENA], F32, c2)
        xnp = sb("xnp", [128, 2, B, PAD + L], F32R, c2)
        c2.close()
        c3 = ExitStack()
        acts.append(sb("acts1", [128, 3, 2, KT, TILE], F32R, c3))
        sb("small1", [128, AO["kq"] - 12288], F32, c3)
        w_f.append(sb("w_f1", [128, 5632], F32R, c3))
        wlow.append(sb("w_low1", [128, 5632], F32R, c3))
        hbuf_1 = sb("hbuf1", [128, 2, TILE], F32, c3)
        sb("paths1", [128, AO["o"] - AO["paths"]], F32, c3)
        fin = sb("fin", [128, 2, TILE], F32, c3)
        sb("oc1", [128, ARENA - AO["oc"]], F32, c3)
        ln_1 = sb("ln1", [128, 8, TILE], F32, c3)
        xn_f.append(xn_1)
        c3.close()

        def at(name, *shape):
            n = 1
            for s in shape:
                n *= s
            v = arena[:, AO[name]:AO[name] + n]
            if len(shape) == 1:
                return v
            names = "abcdef"[:len(shape)]
            return v.rearrange(f"p ({' '.join(names)}) -> p {' '.join(names)}", **dict(zip(names, shape)))

        def ln_bufs(f):
            v = {0: ln_0, 1: ln_1, 2: at("ln", 8, TILE)}[f]
            return {k: v[:, 2 * i:2 * i + 2, :] for i, k in enumerate(("xc", "sq", "y", "u"))}

        gbuf = [ghbuf[:, 0:4], gbuf_1]
        hbuf = [ghbuf[:, 4:6], hbuf_1]
        iobuf = [iobuf_0, iobuf_1]

        kq = at("kq", 2, 16, 128)
        kn = at("kn", 16, 128)
        vb = at("vb", 16, 128)
        vpad = at("vpad", B, HIST + L)
        vt = at("vt", 128, 2, 32)
        ktok = at("ktok", 16, 128)
        vtok = at("vtok", 16, 128)
        alt = at("alt", 2, H, NCH, 2, DH)
        lmat = at("lmat", 2, DH, DH)
        tinv = at("tinv", 2, DH, DH)
        tmp = at("tmp", 1024)
        block = at("block", 2, 8, 2, 128)
        paths = [at("paths", P, 64, DH)[:, p] for p in range(P)]
        kbtok = at("kbtok", 16, 128)
        s_sb = at("ssb", 2, B, 128)
        u_exp = at("uexp", 2, 4, 128)
        w_t = at("wt", 2, 2, 128)
        o_t = at("ot", B * L)
        sq_p = at("sq", 2, 32, DH)
        st = at("st", 64, 32)
        st_t = at("stt", B * L)
        hid = at("hid", 2, 2, TILE)
        lg = at("lg", B * L)
        pl = at("pl", 64, 32)
        o_sq = at("o", 32, DH)
        o_c = at("oc", 2, TILE)
        sm = at("small", 1536)
        qs = at("tinv", 10, TILE)

        names = ("ld_x ld_x2 ld_up ld_hid ld_vec ld_proj ld_gate ld_late ld_w2 ld_t0 ld_t1 st_out "
                 "consts mask_done up_high up_round hid_round ld_h1 h1_round low_1 low_seen conv_round w2_high w2_low vec_act "
                 "pe_a act_a pe_d dve_d dve_lo act_hi act_sq act_t dve_xn xn_pad pad_zero "
                 "act_ss act_nt dve_nrm eye_done inv_done path4 block_zero act_block pe_p dve_u act_u pe_w act_w pe_o act_o "
                 "pe_s dve_s st_zero act_stat dve_stat act_norm path3 st_turned ld_h2 act_exp dve_sub probs mixed mixed_p act_osq dve_ms act_rms "
                 "o_turned dve_step act_step pool_step").split()
        S = {n: sem(n) for n in names}
        x_dram = d["x"].rearrange("(a j p) c -> a p j c", j=4, p=128)
        out_dram = out.rearrange("(x t) c -> x t c", t=64)
        tflat = toep[:, :, :, :, :].rearrange("p a h d x -> p (a h d x)")
        u_sb = tflat[:, 5632:5888].rearrange("p (a b) -> p a b", a=2)
        taps = tflat[:, 0:1536]
        proj = tflat[:, 1536:2048].rearrange("p (i n) -> p i n", i=4)
        conv_s = tflat[:, 2048:2048 + 13 * 128].rearrange("p (i n) -> p i n", i=13)
        gx_s = tflat[:, 3712:3968]
        mtmp = tflat[:, 3968:4224].rearrange("p (a b) -> p a b", a=2)
        lnb = {f: ln_bufs(f) for f in range(3)}
        ex5 = sm[:, 0:320].rearrange("p (a t c) -> p a t c", a=2, c=P)
        pr5 = sm[:, 320:640].rearrange("p (a t c) -> p a t c", a=2, c=P)
        pr64 = sm[:, 320:640].rearrange("p (t c) -> p t c", c=P)
        mx, su = sm[:, 640:672], sm[:, 672:704]
        ms, var, rt, t2 = (sm[:, 704 + 32 * k:736 + 32 * k] for k in range(4))
        ny = at("ny", 4, TILE)
        pall = at("paths", P, 64, DH)

        def low_part(e, f, lo, hi):
            return e.tensor_tensor(wlow[f][:, lo:hi], (wst1, wstage)[f][:, lo:hi], w_f[f][:, lo:hi].bitcast(F32),
                                   ALU.subtract)

        def vc(name, i=0, n=1):
            return vec[:, V[name] + i:V[name] + i + n]

        def tile(ap, t):
            return ap[:, t * TILE:(t + 1) * TILE]

        def quarter(ap, i):
            return ap.rearrange("p (x t) -> p x t", t=64)[:, :, 16 * i:16 * i + 16]

        def x_tile(f, i):
            return quarter(x_t[:, :], i) if f == 1 else tile(x_t, i)

        def like_x(f, ap):
            return ap.rearrange("p (x t) -> p x t", t=16) if f == 1 else ap

        def chunked(ap, t):
            g, o = t // 2, 64 * (t % 2)
            return ap[:, NCH * g:NCH * g + NCH, o:o + 64].rearrange("p n (b t) -> p b n t", b=2)

        def plain(ap):
            return ap.rearrange("p (b n t) -> p b n t", b=2, n=NCH)

        def x_ready(e, f, t):
            if f == 0:
                e.wait_ge(S["act_a"], A_AT[("in", 0, t)] + 1)
            elif f == 2:
                e.wait_ge(S["dve_d"], D_AT[("down", 0, t)] + 1)
            else:
                e.wait_ge(S["dve_d"], D_AT[("wo", 2, t)] + 1)

        def part_entry(e, f):
            if f == 2:
                e.wait_ge(S["dve_d"], D_AT[("down", 0, NT - 1)] + 1)
                e.wait_ge(S["act_a"], A_AT[("gsum", 0, 1)] + 1)
                e.wait_ge(S["conv_round"], 1)

        def set_free(e, j):
            if j >= 3:
                user = USERS[j - 3]
                if user[0] == "down":
                    e.wait_ge(S["pe_d"], D_AT[user] + 1)
                else:
                    e.wait_ge(S["pe_a"], A_AT[user] + KT)

        ENTRY = {("qkv", 2, 0): 2}

        def load_weights(e, stage, first, second, rest):
            e.dma_start(stage[:, 0:512], d["w1"]).then_inc(first, 16)
            e.dma_start(stage[:, 512:1024], d["w2"]).then_inc(first, 16)
            for k, o in (("h1", 1024), ("h2", 3072)):
                e.dma_start(stage[:, o:o + 2048].rearrange("p (k n) -> p k n", k=KT),
                            d[k].rearrange("(k p) n -> p k n", p=128)).then_inc(second if k == "h1" else rest, 16)
            e.dma_start(stage[:, 5120:5632].rearrange("p (k n) -> p k n", k=KT),
                        d["w3"].rearrange("(k p) n -> p k n", p=128)).then_inc(rest, 16)

        def load_toep(e, grp):
            for h in range(H):
                rows = bass.AP(d["fir"].tensor, d["fir"].offset + (4 * h + grp) * 384 * 8, [[24, WIN], [8, WIN], [1, 8]])
                e.dma_start(toep[0:WIN, grp % 2, h], rows).then_inc(S[f"ld_t{grp % 2}"], 16)

        def mixture(e, first, end, own, settle):
            r = slice(first, end)
            w = pr64[:, r].rearrange("p t c -> p c t").unsqueeze(3).to_broadcast([128, P, end - first, DH])
            own(e.tensor_tensor(pall[:, :, r], pall[:, :, r], w, ALU.mult))
            settle()
            own(e.tensor_tensor(pall[:, 0:2, r], pall[:, 0:2, r], pall[:, 2:4, r], ALU.add))
            settle()
            own(e.tensor_tensor(paths[0][:, r], paths[0][:, r], paths[1][:, r], ALU.add))
            settle()
            return e.tensor_tensor(paths[0][:, r], paths[0][:, r], paths[4][:, r], ALU.add)

        blk = ctx.enter_context(nc.Block())

        @blk.sync
        def _(e):
            for a in range(2):
                e.dma_start(iobuf[0][:, a], x_dram[a]).then_inc(S["ld_x"], 16)
            load_weights(e, wst1, S["ld_up"], S["ld_h1"], S["ld_hid"])
            for a in range(2, NT):
                e.dma_start(iobuf[0][:, a], x_dram[a]).then_inc(S["ld_x2"], 16)
            e.dma_start(proj, d["proj"].rearrange("p (i n) -> p i n", i=4)).then_inc(S["ld_proj"], 16)
            e.dma_start(taps, d["taps"].to_broadcast([128, 1536])).then_inc(S["ld_proj"], 16)
            e.dma_start(gx_s, d["gW1"][0:D, :]).then_inc(S["ld_proj"], 16)
            e.dma_start(gate_2[:, :, :], d["gW2"].rearrange("(k p) n -> p k n", p=128)).then_inc(S["ld_late"], 16)
            e.dma_start(wo_w[:, :], d["Wo"]).then_inc(S["ld_late"], 16)
            for pair in range(2):
                if pair:
                    e.wait_ge(S["pe_a"], A_AT[("gsum", 0, 0)] + 1)
                for h2 in range(2):
                    r = D + 128 * (2 * pair + h2)
                    src = bass.AP(d["gW1"].tensor, d["gW1"].offset + r * 2 * D,
                                  [[2 * D, 128], [HID * 2 * D, P], [1, 2 * D]])
                    e.dma_start(g_rows[:, h2], src).then_inc(S["ld_gate"], 16)
            e.wait_ge(S["conv_round"], 1)
            e.wait_ge(S["mask_done"], 1)
            load_toep(e, 0)
            load_toep(e, 1)
            for grp in (2, 3):
                e.wait_ge(S["pe_a"], A_AT[("fir", 2, 4 * (grp - 2) + 3)] + 1)
                load_toep(e, grp)
            e.wait_ge(S["pe_a"], A_AT[("fir", 2, 15)] + 1)
            load_weights(e, wstage, S["ld_w2"], S["ld_h2"], S["ld_h2"])
            for t in range(NT):
                e.wait_ge(S["act_a"], A_AT[("out", 1, t)] + 1)
                for j in range(4):
                    e.dma_start(out_dram[8 * j:8 * j + 8, 16 * t:16 * t + 16, :], iobuf[1][:, t, j]
                                ).then_inc(S["st_out"], 16)
            e.wait_ge(S["st_out"], 16 * 4 * NT)

        @blk.gpsimd
        def _(e):
            step = [0]

            def own(ins):
                step[0] += 1
                ins.then_inc(S["pool_step"], 1)
                e.wait_ge(S["pool_step"], step[0])

            own(e.memset(ident[:, :], 0.0))
            own(e.memset(mean_w[:, :], 1.0 / D))
            own(e.memset(vc("l2eps"), L2_EPS))
            own(e.memset(vc("lneps"), LN_EPS))
            own(e.memset(vc("rmseps"), RMS_EPS))
            e.affine_select(out=ident[:, :], in_=ident[:, :], compare_op=ALU.not_equal, fill=1.0,
                            base=0, pattern=[[-1, 128]], channel_multiplier=1).then_inc(S["consts"], 1)
            own(e.memset(head_w[:, :], 0.0))
            own(e.memset(pick[:, :], 0.0))
            own(e.memset(mtmp, 1.0))
            for q in range(4):
                own(e.memset(head_w[32 * q:32 * q + 32, 32 * q:32 * q + 32], 1.0))
            for which, op in ((0, ALU.is_gt), (1, ALU.is_ge)):
                own(e.affine_select(out=mtmp[:, which], in_=mtmp[:, which], compare_op=op, fill=0.0,
                                    base=0, pattern=[[1, 128]], channel_multiplier=-1))
            for q in range(4):
                own(e.tensor_copy(mask[32 * q:32 * q + 32], mtmp[32 * q:32 * q + 32, :, 32 * q:32 * q + 32]))
            own(e.tensor_copy(pick[:, 16:20], head_w[:, 0:128:32]))
            e.tensor_scalar(pick[:, 16:19], pick[:, 16:19], 1.0 / DH, None, ALU.mult).then_inc(S["mask_done"], 1)
            e.wait_ge(S["up_high"], 1)
            low_part(e, 0, 0, 1024).then_inc(S["up_round"], 1)
            for part, (lo, hi) in enumerate(((1024, 3072), (3072, 5632))):
                e.wait_ge(S["hid_round" if part else "h1_round"], 1)
                low_part(e, 0, lo, hi).then_inc(S["low_1"], 1)
            e.wait_ge(S["pe_a"], A_AT[("up", 0, NT - 1)] + KT)
            e.wait_ge(S["pe_d"], D_AT[("up", 0, NT - 1)] + KT)
            own(e.memset(xnp[:, 0, :, 0:PAD].bitcast(F32), 0.0))
            e.memset(xnp[:, 1, :, 0:PAD].bitcast(F32), 0.0).then_inc(S["xn_pad"], 1)
            part_entry(e, 2)
            own(e.memset(vpad[:, :, 0:HIST], 0.0))
            e.memset(vec[:, 54:55], 0.0).then_inc(S["pad_zero"], 1)
            e.wait_ge(S["dve_nrm"], NT)
            for g in range(2):
                own(e.memset(tinv[:, g], 0.0))
                e.memset(at("tinv", 2, DH * DH)[:, g, 0:DH * DH:DH + 1], 1.0).then_inc(S["eye_done"], 1)
            e.wait_ge(S["pe_a"], A_AT[("fir", 2, 15)] + 1)
            for parity in range(2):
                e.memset(block[:, parity], 0.0).then_inc(S["block_zero"], 1)
            e.memset(at("st", 2048), 0.0).then_inc(S["st_zero"], 1)
            e.wait_ge(S["w2_high"], 1)
            low_part(e, 1, 0, 1024).then_inc(S["w2_low"], 1)
            low_part(e, 1, 1024, 5632).then_inc(S["w2_low"], 1)
            for half in range(2):
                e.wait_ge(S["probs"], half + 1)
                mixture(e, 32 if half else MIX_SPLIT, 64 if half else 32, own, lambda: None
                        ).then_inc(S["mixed_p"], 1)

        @blk.scalar
        def _(e):
            step = [0]

            def own(ins):
                step[0] += 1
                ins.then_inc(S["act_step"], 1)

            def settle():
                e.wait_ge(S["act_step"], step[0])

            e.dma_start(vec[:, 0:NVEC], d["vec"]).then_inc(S["ld_vec"], 16)

            def numbers():
                e.wait_ge(S["ld_vec"], 16)
                own(e.activation(vc("atau"), vc("ltau"), ACT.Abs))
                settle()
                own(e.activation(vc("etau"), vc("atau"), ACT.Exp, scale=-1.0))
                own(e.activation(vc("eeps", 0, P), vc("epsl", 0, P), ACT.Exp, scale=-1.0))
                settle()
                e.activation(vc("lntau"), vc("etau"), ACT.Ln, bias=1.0).then_inc(S["vec_act"], 1)

            def blocks(n):
                if n >= 2:
                    e.wait_ge(S["pe_o"], 2 * (n - 1))
                for q in range(4):
                    r = slice(32 * q, 32 * q + 32)
                    e.activation(block[r, n % 2, :, :, r], alt[r, :, :, n].rearrange("p g h a t -> p (g h) a t"),
                                 ACT.Copy).then_inc(S["act_block"], 1)

            def plain_u(n, g):
                e.wait_ge(S["dve_u"], 2 * n + g + 1)
                if n:
                    e.wait_ge(S["pe_o"], 2 * (n - 1) + g + 1)
                e.activation(u_sb[:, g], ps_a[g][:, 0:128], ACT.Copy).then_inc(S["act_u"], 1)

            def output(n, g):
                e.wait_ge(S["pe_o"], 2 * n + g + 1)
                dst = o_t[:, :].rearrange("p (b t) -> p b t", b=B)[:, 4 * g:4 * g + 4, DH * n:DH * n + DH]
                e.activation(dst, ps_a[2 + g][:, 0:128].rearrange("p (b t) -> p b t", b=4), ACT.Copy
                             ).then_inc(S["act_o"], 1)

            def squares(q):
                if q >= 2:
                    e.wait_ge(S["dve_stat"], q - 1)
                p, half = STAT_ORDER[q // 2], q % 2
                if p == 4:
                    e.wait_ge(S["path4"], 1)
                e.activation(sq_p[:, half], paths[p][:, 32 * half:32 * half + 32], ACT.Square
                             ).then_inc(S["act_stat"], 1)

            for s in STEPS:
                kind, f, i = s
                a, dd = A_AT[s], D_AT[s]
                bank = ps_a[a % NRING]
                if s in ENTRY:
                    part_entry(e, ENTRY[s])
                if kind == "in":
                    e.wait_ge(S["pe_a"], a + 1)
                    e.activation(tile(x_t, i), bank[:, :], ACT.Copy).then_inc(S["act_a"], 1)
                    if s == ("in", 0, 1):
                        e.wait_ge(S["ld_up"], 32)
                        e.activation(w_f[0][:, 0:1024], wst1[:, 0:1024], ACT.Copy).then_inc(S["up_high"], 1)
                elif kind == "gsum":
                    r = slice(64 * i, 64 * i + 64)
                    e.wait_ge(S["pe_a"], a + 1)
                    e.activation(gate_s[r, :], bank[r, 0:2 * D], ACT.Copy).then_inc(S["act_a"], 1)
                elif kind == "mean":
                    n = NORM_AT[s]
                    if n >= 2:
                        e.wait_ge(S["dve_xn"], n - 1)
                    e.wait_ge(S["dve_d"], dd + 1)
                    e.activation(lnb[f]["sq"][:, i % 2], lnb[f]["xc"][:, i % 2], ACT.Square).then_inc(S["act_sq"], 1)
                elif kind == "var":
                    e.wait_ge(S["pe_d"], dd + 1)
                    own(e.activation(lnb[f]["y"][:, i % 2], ps_d[:, dd % NRING], ACT.Abs_reciprocal_sqrt,
                                     bias=vc("lneps")))
                    settle()
                    e.activation(lnb[f]["sq"][:, i % 2], lnb[f]["y"][:, i % 2], ACT.Square).then_inc(S["act_t"], 1)
                    if s == ("var", 0, 1):
                        e.wait_ge(S["ld_h1"], 16)
                        e.activation(w_f[0][:, 1024:3072], wst1[:, 1024:3072], ACT.Copy).then_inc(S["h1_round"], 1)
                        e.wait_ge(S["ld_hid"], 32)
                        e.activation(w_f[0][:, 3072:5632], wst1[:, 3072:5632], ACT.Copy).then_inc(S["hid_round"], 1)
                elif kind == "up":
                    j = SET_AT[s]
                    if s == ("up", 0, 0):
                        e.wait_ge(S["ld_vec"], 16)
                    if s == ("up", 1, 0):
                        e.wait_ge(S["w2_low"], 2)
                    set_free(e, j)
                    for m in range(KT + 1):
                        if m < KT:
                            gi = KT * j + m
                            e.wait_ge(S["pe_a"], a + m + 1)
                            if gi >= 4:
                                e.wait_ge(S["dve_lo"], gi - 3)
                            e.activation(gbuf[f][:, gi % 4], ps_a[(a + m) % NRING][:, :], ACT.Silu,
                                         scale=vc("s1", m)).then_inc(S["act_a"], 1)
                        if m:
                            e.wait_ge(S["dve_d"], dd + m)
                            e.activation(acts[f][:, j % 3, 0, m - 1], hbuf[f][:, (m - 1) % 2], ACT.Copy
                                         ).then_inc(S["act_hi"], 1)
                elif s == ("inverse", 2, 1):
                    numbers()
                elif kind in ("hid1", "hid2"):
                    j = SET_AT[s]
                    set_free(e, j)
                    for m in range(KT):
                        gi = KT * j + m
                        sc = vc("g1" if kind == "hid1" else "g2", m)
                        e.wait_ge(S["pe_a"], a + m + 1)
                        e.wait_ge(S["dve_lo"], gi - 3)
                        src = ps_a[(a + m) % NRING]
                        e.activation(gbuf[f][:, gi % 4], src[:, :], ACT.Gelu, scale=sc).then_inc(S["act_step"], 1)
                        step[0] += 1
                        e.activation(acts[f][:, j % 3, 0, m], src[:, :], ACT.Gelu, scale=sc).then_inc(S["act_a"], 1)
                elif kind == "qkv":
                    k2 = i % 2
                    if i >= 2:
                        e.wait_ge(S["dve_nrm"], i - 1)
                    else:
                        e.wait_ge(S["pad_zero"], 1)
                    for w in range(4):
                        e.wait_ge(S["pe_a"], a + w + 1)
                        src = ps_a[(a + w) % NRING][:, :]
                        if w == 2:
                            e.activation(vpad[:, 2 * i:2 * i + 2, HIST:HIST + L],
                                         src.rearrange("p (b t) -> p b t", b=2), ACT.Silu).then_inc(S["act_a"], 1)
                        elif w == 3:
                            e.activation(qs[:, 4 + k2], src, ACT.Tanh, scale=0.5).then_inc(S["act_a"], 1)
                        else:
                            e.activation(qs[:, 2 * w + k2], src, ACT.Silu).then_inc(S["act_a"], 1)
                    e.wait_ge(S["act_a"], a + 2)
                    for w in range(2):
                        e.activation(qs[:, 6 + 2 * w + k2], qs[:, 2 * w + k2], ACT.Square).then_inc(S["act_ss"], 1)
                elif kind == "sumsq":
                    for w in range(2):
                        y = ny[:, 2 * w + i % 2]
                        e.wait_ge(S["pe_d"], dd + w + 1)
                        own(e.activation(y, ps_d[:, (dd + w) % NRING], ACT.Abs_reciprocal_sqrt, bias=vc("l2eps")))
                        settle()
                        e.activation(qs[:, 6 + 2 * w + i % 2], y, ACT.Square).then_inc(S["act_nt"], 1)
                elif kind in ("window", "token"):
                    e.wait_ge(S["pe_a"], a + 1)
                    if kind == "window":
                        half, b = i // 8, i % 8
                        e.activation(vt[0:WIN, :, half, 4 * b:4 * b + 4].rearrange("p c w -> p w c"),
                                     bank[0:WIN, :].rearrange("p (w c) -> p w c", w=4), ACT.Copy
                                     ).then_inc(S["act_a"], 1)
                    else:
                        dst = (ktok, vtok, kbtok)[i // 4][:, 4 * (i % 4):4 * (i % 4) + 4, :]
                        e.activation(dst, bank[:, :].rearrange("p (g c) -> p g c", g=4), ACT.Copy
                                     ).then_inc(S["act_a"], 1)
                elif kind == "fir":
                    e.wait_ge(S["pe_a"], a + 1)
                    dst = pall[:, 0:3, :, 2 * i:2 * i + 2][:, :, ::-1, :].rearrange("p f t c -> p c t f")
                    e.activation(dst, bank[:, 0:384].rearrange("p (c x f) -> p c x f", c=2, x=64), ACT.Copy
                                 ).then_inc(S["act_a"], 1)
                elif kind == "chain":
                    n = i
                    if n == 0:
                        e.wait_ge(S["block_zero"], 1)
                        e.wait_ge(S["inv_done"], 2)
                        blocks(0)
                    plain_u(n, 0)
                    if n == 0:
                        e.wait_ge(S["block_zero"], 2)
                    if n + 1 < NCH:
                        blocks(n + 1)
                    if n:
                        output(n - 1, 1)
                    plain_u(n, 1)
                    output(n, 0)
                    if n + 1 < NCH:
                        for g in range(2):
                            e.wait_ge(S["pe_w"], 2 * n + g + 1)
                            if n >= 2:
                                e.wait_ge(S["pe_p"], 2 * (n - 1) + g + 1)
                            e.activation(w_t[:, (n + 1) % 2, g], ps_d[:, 2 + g, 0:128], ACT.Copy, scale=-1.0
                                         ).then_inc(S["act_w"], 1)
                    else:
                        output(n, 1)
                    squares(n)
                elif kind == "stats":
                    for half in range(2):
                        e.wait_ge(S["path3"], half + 1)
                        squares(NCH + half)
                    for half in range(2):
                        r = slice(32 * half, 32 * half + 32)
                        e.wait_ge(S["dve_stat"], NCH + half + 1)
                        e.activation(st[:, r, 3:4 * P:4], st[:, r, 1:4 * P:4], ACT.Sqrt).then_inc(S["act_norm"], 1)
                        if half == 0:
                            e.wait_ge(S["ld_w2"], 32)
                            e.wait_ge(S["ld_h2"], 48)
                            e.activation(w_f[1][:, :], wstage[:, :], ACT.Copy).then_inc(S["w2_high"], 1)
                elif kind == "gate":
                    if i >= 2:
                        e.wait_ge(S["pe_d"], D_AT[("logit", 2, i - 2)] + 1)
                    for m in range(2):
                        e.wait_ge(S["pe_a"], a + m + 1)
                        e.activation(hid[:, i % 2, m], ps_a[(a + m) % NRING][:, :], ACT.Gelu,
                                     bias=vc("gb1", m)).then_inc(S["act_a"], 1)
                elif kind == "soft":
                    e.wait_ge(S["dve_sub"], i + 1)
                    e.activation(ex5[:, i], ex5[:, i], ACT.Exp).then_inc(S["act_exp"], 1)
                elif kind == "scale":
                    e.wait_ge(S["mixed"], 1)
                    e.wait_ge(S["mixed_p"], i + 1)
                    e.activation(o_sq, paths[0][:, 32 * i:32 * i + 32], ACT.Square).then_inc(S["act_osq"], 1)
                    e.wait_ge(S["dve_ms"], i + 1)
                    e.activation(rt, var, ACT.Abs_reciprocal_sqrt).then_inc(S["act_rms"], 1)
                elif kind == "out":
                    e.wait_ge(S["pe_a"], a + 1)
                    e.activation(iobuf[1][:, i], bank[:, :].rearrange("p (j c) -> p j c", j=4), ACT.Copy
                                 ).then_inc(S["act_a"], 1)

        @blk.tensor
        def _(e):
            state = dict(chain_over=False)

            def take_a(n):
                if state["chain_over"]:
                    state["chain_over"] = False
                    e.wait_ge(S["act_o"], 2 * NCH)
                    e.wait_ge(S["dve_s"], 2 * (NCH - 1))
                    e.wait_ge(S["act_w"], 2 * (NCH - 1))
                if n >= NRING:
                    e.wait_ge(S["act_a"], n - NRING + 1)
                return ps_a[n % NRING]

            def take_d(n):
                if n >= NRING:
                    e.wait_ge(S["dve_d"], n - NRING + 1)
                return ps_d[:, n % NRING]

            any_low = {}

            def if_low(which, layer, s):
                with e.If(any_low[which] > 0):
                    layer(s, True)
                with e.If(any_low[which] < 1):
                    layer(s, False)

            def products(bank, f, r, acts_hi, acts_lo, low, start, stop):
                if low:
                    e.matmul(bank, wlow[f][:, r], acts_hi, start=start, stop=False)
                e.matmul(bank, w_f[f][:, r], acts_hi, start=start and not low, stop=False)
                return e.matmul(bank, w_f[f][:, r], acts_lo, start=False, stop=stop)

            def up(s, low):
                kind, f, i = s
                x = xn_f[f][:, i % 2]
                for m in range(KT):
                    for bank, o, done in ((take_a(A_AT[s] + m)[:, :], 0, "pe_a"), (take_d(D_AT[s] + m), 512, "pe_d")):
                        r = slice(o + 128 * m, o + 128 * m + 128)
                        products(bank, f, r, x[:, 0], x[:, 1], low, True, True).then_inc(S[done], 1)

            def down(s, low):
                kind, f, i = s
                c, bank = USED_AT[s], take_d(D_AT[s])
                x = acts[f][:, c % 3]
                for k in range(KT):
                    e.wait_ge(S["dve_lo"], KT * c + k + 1)
                    r = slice(5120 + 128 * k, 5120 + 128 * k + 128)
                    last = products(bank, f, r, x[:, 0, k], x[:, 1, k], low, k == 0, k == KT - 1)
                last.then_inc(S["pe_d"], 1)

            def hidden(s, low):
                kind, f, i = s
                a, c = A_AT[s], USED_AT[s]
                o = 1024 if kind == "hid1" else 3072
                for m in range(KT):
                    bank = take_a(a + m)
                    for k in range(KT):
                        if m == 0:
                            e.wait_ge(S["dve_lo"], KT * c + k + 1)
                        r = slice(o + 512 * k + 128 * m, o + 512 * k + 128 * m + 128)
                        last = products(bank[:, :], f, r, acts[f][:, c % 3, 0, k], acts[f][:, c % 3, 1, k], low,
                                        k == 0, k == KT - 1)
                    last.then_inc(S["pe_a"], 1)

            def start_u(n, g):
                e.wait_ge(S["act_block"], 4 * (n + 1))
                if n:
                    e.wait_ge(S["act_u"], 2 * (n - 1) + g + 1)
                for h in range(H):
                    c = slice(32 * h, 32 * h + 32)
                    last = e.matmul(ps_a[g][:, c], block[:, n % 2, 4 * g + h, 0, :], vtok[:, NCH * g + n, c],
                                    start=h == 0, stop=not n, skip_group_check=True)
                if not n:
                    last.then_inc(S["pe_p"], 1)

            def finish_u(n, g):
                e.wait_ge(S["dve_s"], 2 * (n - 1) + g + 1)
                e.wait_ge(S["act_w"], 2 * (n - 1) + g + 1)
                for b in range(4):
                    c = slice(32 * b, 32 * b + 32)
                    last = e.matmul(ps_a[g][c, 0:128], w_t[:, n % 2, g, c], s_sb[:, (n - 1) % 2, 4 * g + b, :],
                                    start=False, stop=True, skip_group_check=True)
                last.then_inc(S["pe_p"], 1)

            def next_s(n, g):
                e.wait_ge(S["dve_u"], 2 * n + g + 1)
                e.matmul(ps_d[:, g, :].rearrange("p (b c) -> p b c", b=4), ktok[:, NCH * g + n, :], u_exp[:, g],
                         start=n == 0, stop=True, skip_group_check=True).then_inc(S["pe_s"], 1)

            def output(n, g):
                e.wait_ge(S["act_u"], 2 * n + g + 1)
                if n:
                    e.wait_ge(S["act_o"], 2 * (n - 1) + g + 1)
                for h in range(H):
                    c = slice(32 * h, 32 * h + 32)
                    last = e.matmul(ps_a[2 + g][c, 0:128], u_sb[:, g, c], block[:, n % 2, 4 * g + h, 1, :],
                                    start=True, stop=not n, skip_group_check=True)
                if n:
                    for b in range(4):
                        c = slice(32 * b, 32 * b + 32)
                        last = e.matmul(ps_a[2 + g][:, c], s_sb[:, (n - 1) % 2, 4 * g + b, :],
                                        kq[:, 1, NCH * g + n, c], start=False, stop=True, skip_group_check=True)
                last.then_inc(S["pe_o"], 1)

            e.wait_ge(S["consts"], 1)
            for s in STEPS:
                kind, f, i = s
                a, dd = A_AT[s], D_AT[s]
                if kind == "in":
                    e.wait_ge(S["ld_x" if i < 2 else "ld_x2"], 32)
                    bank = take_a(a)
                    for j in range(4):
                        last = e.transpose(bank[:, 128 * j:128 * j + 128], iobuf[0][:, i, j, :], ident[:, :])
                    last.then_inc(S["pe_a"], 1)
                elif kind == "gsum":
                    bank = take_a(a)
                    e.wait_ge(S["ld_gate"], 32 * (i + 1))
                    e.wait_ge(S["mask_done"], 1)
                    for p in range(P):
                        for h2 in range(2):
                            r = slice(64 * i + 32 * h2, 64 * i + 32 * h2 + 32)
                            last = e.matmul(bank[r, 0:2 * D], pick[:, 16 - 4 * p:48 - 4 * p], g_rows[:, h2, p],
                                            start=p == 0, stop=p == P - 1)
                    last.then_inc(S["pe_a"], 1)
                elif kind == "mean":
                    x_ready(e, f, i)
                    e.matmul(like_x(f, take_d(dd)), mean_w[:, :], x_tile(f, i), start=True, stop=True
                             ).then_inc(S["pe_d"], 1)
                elif kind == "var":
                    e.wait_ge(S["act_sq"], NORM_AT[("mean", f, i)] + 1)
                    e.matmul(take_d(dd), mean_w[:, :], lnb[f]["sq"][:, i % 2], start=True, stop=True
                             ).then_inc(S["pe_d"], 1)
                elif kind == "up":
                    if i == 0:
                        e.wait_ge(S["up_round" if f == 0 else "w2_low"], 1)
                    e.wait_ge(S["dve_xn"], VAR_AT[("var", f, i)] + 1)
                    if s in (("up", 0, 0), ("up", 0, 1)):
                        up(s, True)
                    else:
                        if_low("hid1", up, s)
                elif kind in ("hid1", "hid2"):
                    if kind == "hid1" and i == 0:
                        e.wait_ge(S["w2_low" if f else "h1_round"], 2 if f else 1)
                    if s == ("hid2", 0, 0):
                        e.wait_ge(S["hid_round"], 1)
                    if s == ("hid1", 0, 0):
                        e.wait_ge(S["low_1"], 1)
                        hidden(s, True)
                    else:
                        if_low(kind, hidden, s)
                elif kind == "flag":
                    e.wait_ge(S["low_seen"], i + 1)
                    e.matmul(take_d(dd)[:, 0:1], mean_w[:, :], low_max[:, i:i + 1], start=True, stop=True
                             ).then_inc(S["pe_d"], 1)
                    e.wait_ge(S["dve_d"], dd + 1)
                    any_low["hid1" if i == 0 else "hid2"] = e.value_load(low_any[0:1, i:i + 1], min_val=0, max_val=1)
                elif kind == "down":
                    if_low("hid2", down, s)
                elif kind == "qkv":
                    if i == 0:
                        e.wait_ge(S["xn_pad"], 1)
                    e.wait_ge(S["dve_xn"], VAR_AT[("var", 2, i)] + 1)
                    for w in range(4):
                        bank = take_a(a + w)[:, :].rearrange("p (b t) -> p b t", b=2)
                        todo = [(w * TAPS + j, 1 + j) for j in range(TAPS)] if w < 3 else [(12, PAD)]
                        todo = [(ww, o, hw, hx) for ww, o in todo for hw, hx in ((0, 0), (0, 1), (1, 0))]
                        for n, (ww, o, hw, hx) in enumerate(todo):
                            last = e.matmul(bank, conv_w[:, hw, ww], xnp[:, hx, 2 * i:2 * i + 2, o:o + L],
                                            start=n == 0, stop=n == len(todo) - 1)
                        last.then_inc(S["pe_a"], 1)
                elif kind == "sumsq":
                    for w in range(2):
                        e.wait_ge(S["act_ss"], 2 * i + w + 1)
                        e.matmul(take_d(dd + w), head_w[:, :], qs[:, 6 + 2 * w + i % 2], start=True, stop=True
                                 ).then_inc(S["pe_d"], 1)
                elif kind in ("window", "token"):
                    if s == ("window", 2, 0):
                        e.wait_ge(S["act_a"], A_AT[("qkv", 2, NT - 1)] + 3)
                        e.wait_ge(S["pad_zero"], 1)
                    bank = take_a(a)
                    for w in range(4):
                        if kind == "window":
                            o = DH * (2 * w + i // 8)
                            last = e.transpose(bank[0:WIN, 128 * w:128 * w + 128], vpad[:, i % 8, o:o + WIN], ident[:, :])
                        else:
                            src = (kn, vb, kq[:, 0])[i // 4][:, 4 * (i % 4) + w, :]
                            last = e.transpose(bank[:, 128 * w:128 * w + 128], src, ident[:, :])
                    last.then_inc(S["pe_a"], 1)
                elif kind == "gram":
                    e.wait_ge(S["dve_nrm"], NT * (i + 1) // 2)
                    for h in range(H):
                        bank = take_d(dd + h)
                        r = slice(32 * h, 32 * h + 32)
                        for n in range(NCH):
                            for b in range(4):
                                c = slice(32 * b, 32 * b + 32)
                                last = e.matmul(bank[c, 64 * n:64 * n + 64].rearrange("p (a t) -> p a t", a=2),
                                                kn[r, NCH * i + n, c], kq[r, :, NCH * i + n, c],
                                                start=True, stop=True)
                        last.then_inc(S["pe_d"], 1)
                elif kind == "fir":
                    grp = i // 4
                    if i == 0:
                        e.wait_ge(S["act_a"], A_AT[("token", 2, 11)])
                    if i % 4 == 0:
                        e.wait_ge(S[f"ld_t{grp % 2}"], 64 * (grp // 2 + 1))
                    bank = take_a(a)
                    for c2 in range(2):
                        for half in range(2):
                            for h in range(H):
                                dl = (2 * i + c2) % 8
                                o = 192 * c2 + WIN * (1 - half)
                                last = e.matmul(bank[32 * h:32 * h + 32, o:o + WIN],
                                                vt[0:WIN, DH * h + 2 * i + c2, half, :], toep[0:WIN, grp % 2, h, :, dl],
                                                start=True, stop=True)
                    last.then_inc(S["pe_a"], 1)
                elif kind == "chain":
                    n = i
                    if n == 0:
                        e.wait_ge(S["act_a"], a)
                        e.wait_ge(S["dve_d"], dd)
                        start_u(0, 0)
                        start_u(0, 1)
                    else:
                        finish_u(n, 0)
                        output(n - 1, 1)
                    if n < NCH - 1:
                        next_s(n, 0)
                    if n:
                        finish_u(n, 1)
                    output(n, 0)
                    if n < NCH - 1:
                        next_s(n, 1)
                        for g in range(2):
                            e.wait_ge(S["act_block"], 4 * (n + 2))
                            if n:
                                e.wait_ge(S["act_w"], 2 * (n - 1) + g + 1)
                            for h in range(H):
                                c = slice(32 * h, 32 * h + 32)
                                last = e.matmul(ps_d[c, 2 + g, 0:128], kbtok[:, NCH * g + n + 1, c],
                                                block[:, (n + 1) % 2, 4 * g + h, 0, :], start=True, stop=True)
                            last.then_inc(S["pe_w"], 1)
                        start_u(n + 1, 0)
                        start_u(n + 1, 1)
                    else:
                        output(n, 1)
                    state["chain_over"] = n == NCH - 1
                elif kind == "gate":
                    e.wait_ge(S["st_turned"], i + 1)
                    for m in range(2):
                        c = slice(128 * m, 128 * m + 128)
                        bank = take_a(a + m)[:, :]
                        for n, (hw, hx) in enumerate(((0, 0), (0, 1), (1, 0))):
                            e.matmul(bank.rearrange("p (b w t) -> p b w t", b=B, t=16), gate_x[:, hw, c],
                                     xnp[:, hx, :, PAD:PAD + L].rearrange("p b (w t) -> p b w t", t=64)[
                                         :, :, :, 16 * i:16 * i + 16], start=n == 0, stop=False)
                        e.matmul(bank.rearrange("p (x t) -> p x t", t=16), gate_s[:, c], quarter(st_t, i),
                                 start=False, stop=True).then_inc(S["pe_a"], 1)
                elif kind == "logit":
                    bank = take_d(dd)
                    if i == 0:
                        e.wait_ge(S["ld_late"], 32)
                    for m in range(2):
                        e.wait_ge(S["act_a"], A_AT[("gate", 2, i)] + m + 1)
                        last = e.matmul(bank, gate_2[:, m, :], hid[:, i % 2, m], start=m == 0, stop=m == 1)
                    last.then_inc(S["pe_d"], 1)
                elif kind == "wo":
                    e.wait_ge(S["o_turned"], i + 1)
                    e.matmul(take_d(dd), wo_w[:, :], o_c[:, i % 2], start=True, stop=True).then_inc(S["pe_d"], 1)
                elif kind == "out":
                    e.wait_ge(S["dve_d"], D_AT[("down", 1, i)] + 1)
                    bank = take_a(a)
                    for j in range(4):
                        last = e.transpose(bank[:, 128 * j:128 * j + 128], fin[:, i % 2, 128 * j:128 * j + 128], ident[:, :])
                    last.then_inc(S["pe_a"], 1)

        @blk.vector
        def _(e):
            step = [0]

            def own(ins):
                step[0] += 1
                ins.then_inc(S["dve_step"], 1)

            def settle():
                e.wait_ge(S["dve_step"], step[0])

            def numbers():
                e.wait_ge(S["vec_act"], 1)
                own(e.tensor_scalar(vc("mtau"), vc("ltau"), 0.0, 0.5, ALU.max, ALU.add))
                own(e.tensor_scalar(vc("epsd", 0, P), vc("eeps", 0, P), 1.0, 5.0, ALU.add, ALU.mult))
                settle()
                own(e.tensor_tensor(vc("mtau"), vc("mtau"), vc("lntau"), ALU.add))
                own(e.reciprocal(vc("eps", 0, P), vc("epsd", 0, P)))
                settle()
                own(e.reciprocal(vc("itau"), vc("mtau")))
                own(e.tensor_reduce(vc("rest"), vc("eps", 0, P), AX_X, ALU.add))
                settle()
                own(e.tensor_scalar(vc("rest"), vc("rest"), -1.0, 1.0, ALU.mult, ALU.add))

            def projections():
                e.wait_ge(S["ld_proj"], 48)
                for w in range(3):
                    own(e.tensor_tensor(conv_s[:, TAPS * w:TAPS * w + TAPS],
                                        taps[:, 512 * w:512 * w + 512].rearrange("p (j n) -> p j n", j=TAPS),
                                        proj[:, w:w + 1, :].to_broadcast([128, TAPS, 128]), ALU.mult))
                own(e.tensor_copy(conv_s[:, 12], proj[:, 3]))
                own(e.tensor_copy(gate_x[:, 0], gx_s))
                settle()
                own(e.tensor_copy(conv_w[:, 0], conv_s))
                own(e.tensor_tensor(gate_x[:, 1], gx_s, gate_x[:, 0].bitcast(F32), ALU.subtract))
                settle()
                e.tensor_tensor(conv_w[:, 1], conv_s, conv_w[:, 0].bitcast(F32), ALU.subtract
                                ).then_inc(S["conv_round"], 1)
                e.wait_ge(S["ld_late"], 32)
                own(e.tensor_scalar(wo_w[:, :], wo_w[:, :], vc("norm"), None, ALU.mult))

            def refine(bank, t, y, src, eps, free):
                e.scalar_tensor_tensor(out=t, in0=bank, scalar=eps, in1=t, op0=ALU.add, op1=ALU.mult
                                       ).then_inc(S["dve_d"], 1)
                own(e.tensor_tensor(src, src, y, ALU.mult))
                free()
                own(e.tensor_scalar(t, t, -0.5, 1.5, ALU.mult, ALU.add))
                settle()

            def spread_u(n, g):
                e.wait_ge(S["pe_p"], 2 * n + g + 1)
                e.tensor_tensor(u_exp[:, g], ps_a[g][:, 0:128].unsqueeze(1).to_broadcast([128, 4, 128]),
                                head_w[:, 0:128:32].unsqueeze(2).to_broadcast([128, 4, 128]), ALU.mult
                                ).then_inc(S["dve_u"], 1)

            def mask_s(n, g):
                e.wait_ge(S["pe_s"], 2 * n + g + 1)
                if n:
                    e.wait_ge(S["pe_o"], 2 * (n - 1) + g + 1)
                e.tensor_tensor(s_sb[:, n % 2, 4 * g:4 * g + 4, :], ps_d[:, g, :].rearrange("p (b c) -> p b c", b=4),
                                head_w[:, :].unsqueeze(1).to_broadcast([128, 4, 128]), ALU.mult
                                ).then_inc(S["dve_s"], 1)

            def sums(q):
                p, r = STAT_ORDER[q // 2], slice(32 * (q % 2), 32 * (q % 2) + 32)
                own(e.tensor_reduce(st[:, r, 4 * p], paths[p][:, r], AX_X, ALU.add))

            def turn_stats(half):
                e.wait_ge(S["act_norm"], half + 1)
                settle()
                for q in (2 * half, 2 * half + 1):
                    r = slice(16 * q, 16 * q + 16)
                    e.transpose(st_t[:, :].rearrange("p (x t) -> p t x", t=64)[:, r],
                                st[:, r].rearrange("p t c -> p (t c)")).then_inc(S["st_turned"], 1)

            def absolute_sums(q):
                p, r = STAT_ORDER[q // 2], slice(32 * (q % 2), 32 * (q % 2) + 32)
                own(e.tensor_reduce(st[:, r, 4 * p + 2], paths[p][:, r], AX_X, ALU.add, apply_absolute_value=True))

            def square_sums(q):
                p, r = STAT_ORDER[q // 2], slice(32 * (q % 2), 32 * (q % 2) + 32)
                e.wait_ge(S["act_stat"], q + 1)
                e.tensor_reduce(st[:, r, 4 * p + 1], sq_p[:, q % 2], AX_X, ALU.add).then_inc(S["dve_stat"], 1)

            for s in STEPS:
                kind, f, i = s
                a, dd = A_AT[s], D_AT[s]
                if s in ENTRY:
                    part_entry(e, ENTRY[s])
                if kind == "mean":
                    e.wait_ge(S["pe_d"], dd + 1)
                    x_ready(e, f, i)
                    if NORM_AT[s] >= 2:
                        e.wait_ge(S["act_t"], NORM_AT[s] - 1)
                    e.tensor_tensor(like_x(f, lnb[f]["xc"][:, i % 2]), x_tile(f, i), like_x(f, ps_d[:, dd % NRING]),
                                    ALU.subtract).then_inc(S["dve_d"], 1)
                elif kind == "var":
                    b = {k: v[:, i % 2] for k, v in lnb[f].items()}
                    e.wait_ge(S["act_t"], VAR_AT[s] + 1)
                    refine(ps_d[:, dd % NRING], b["sq"], b["y"], b["xc"], LN_EPS,
                           lambda: e.wait_ge(S["dve_d"], dd + 1))
                    own(e.tensor_tensor(b["u"], b["xc"], b["sq"], ALU.mult))
                    settle()
                    if s == ("var", 2, 0):
                        e.wait_ge(S["pe_a"], A_AT[("up", 0, NT - 1)] + KT)
                        e.wait_ge(S["pe_d"], D_AT[("up", 0, NT - 1)] + KT)
                    if f == 2:
                        hi, lo = (xnp[:, part, 2 * i:2 * i + 2, PAD:PAD + L] for part in range(2))
                        u = b["u"].rearrange("p (b t) -> p b t", b=2)
                    else:
                        if i >= 2:
                            e.wait_ge(S["pe_d"], D_AT[("up", f, i - 2)] + KT)
                        if s == ("var", 1, 0):
                            e.wait_ge(S["w2_low"], 2)
                        hi, lo, u = xn_f[f][:, i % 2, 0], xn_f[f][:, i % 2, 1], b["u"]
                    own(e.tensor_copy(hi, u))
                    settle()
                    e.tensor_tensor(lo, u, hi.bitcast(F32), ALU.subtract).then_inc(S["dve_xn"], 1)
                elif kind == "up":
                    j = SET_AT[s]
                    set_free(e, j)
                    for m in range(KT + 1):
                        if m < KT:
                            e.wait_ge(S["pe_d"], dd + m + 1)
                            e.wait_ge(S["act_a"], a + m + 1)
                            if KT * j + m >= 2:
                                e.wait_ge(S["dve_lo"], KT * j + m - 1)
                            e.scalar_tensor_tensor(out=hbuf[f][:, m % 2], in0=ps_d[:, (dd + m) % NRING],
                                                   scalar=vc("s2", m), in1=gbuf[f][:, (KT * j + m) % 4],
                                                   op0=ALU.mult, op1=ALU.mult).then_inc(S["dve_d"], 1)
                        if m:
                            e.wait_ge(S["act_hi"], UP_AT[s] * KT + m)
                            e.tensor_tensor(acts[f][:, j % 3, 1, m - 1], hbuf[f][:, (m - 1) % 2],
                                            acts[f][:, j % 3, 0, m - 1].bitcast(F32), ALU.subtract
                                            ).then_inc(S["dve_lo"], 1)
                    if s == ("up", 0, 0):
                        e.wait_ge(S["low_1"], 1)
                        e.tensor_reduce(low_max[:, 0:1], wlow[0][:, 1024:3072].bitcast(F32), AX_X, ALU.max,
                                        apply_absolute_value=True).then_inc(S["low_seen"], 1)
                    if s == ("up", 0, 1):
                        e.wait_ge(S["low_1"], 2)
                        own(e.tensor_reduce(low_max[:, 1:2], wlow[0][:, 3072:5632].bitcast(F32), AX_X, ALU.max,
                                            apply_absolute_value=True))
                        own(e.tensor_reduce(low_max[:, 2:3], wlow[0][:, 0:1024].bitcast(F32), AX_X, ALU.max,
                                            apply_absolute_value=True))
                        settle()
                        e.tensor_tensor(low_max[:, 1:2], low_max[:, 1:2], low_max[:, 2:3], ALU.max
                                        ).then_inc(S["low_seen"], 1)
                    if s == ("up", 0, 1):
                        own(e.tensor_scalar(vc("s3h"), vc("s3"), 0.5, None, ALU.mult))
                elif kind == "flag":
                    e.wait_ge(S["pe_d"], dd + 1)
                    e.tensor_scalar(low_any[:, i:i + 1], ps_d[:, dd % NRING, 0:1], 0.0, None, ALU.is_gt
                                    ).then_inc(S["dve_d"], 1)
                elif kind in ("hid1", "hid2"):
                    j = SET_AT[s]
                    for m in range(KT):
                        e.wait_ge(S["act_a"], a + m + 1)
                        e.tensor_tensor(acts[f][:, j % 3, 1, m], gbuf[f][:, (KT * j + m) % 4],
                                        acts[f][:, j % 3, 0, m].bitcast(F32), ALU.subtract).then_inc(S["dve_lo"], 1)
                    if s == ("hid2", 0, 1):
                        projections()
                elif kind == "down":
                    e.wait_ge(S["pe_d"], dd + 1)
                    if f == 1 and i >= 2:
                        e.wait_ge(S["pe_a"], A_AT[("out", 1, i - 2)] + 1)
                    e.scalar_tensor_tensor(out=like_x(f, fin[:, i % 2] if f == 1 else tile(x_t, i)),
                                           in0=like_x(f, ps_d[:, dd % NRING]), scalar=vc("s3h"), in1=x_tile(f, i),
                                           op0=ALU.mult, op1=ALU.add).then_inc(S["dve_d"], 1)
                elif kind == "sumsq":
                    k2 = i % 2
                    e.wait_ge(S["act_a"], A_AT[("qkv", 2, i)] + 4)
                    own(e.tensor_scalar(qs[:, 4 + k2], qs[:, 4 + k2], 0.5, 0.5, ALU.mult, ALU.add))
                    settle()
                    beta = qs[:, 4 + k2].rearrange("p (b t) -> p b t", b=2)
                    own(e.tensor_tensor(chunked(vb, i),
                                        vpad[:, 2 * i:2 * i + 2, HIST:HIST + L].rearrange("p b (n t) -> p b n t", n=NCH),
                                        plain(qs[:, 4 + k2]), ALU.mult))
                    for w in range(2):
                        src, t, y = qs[:, 2 * w + k2], qs[:, 6 + 2 * w + k2], ny[:, 2 * w + k2]
                        e.wait_ge(S["act_nt"], 2 * i + w + 1)
                        refine(ps_d[:, (dd + w) % NRING], t, y, src, L2_EPS,
                               lambda: e.wait_ge(S["dve_d"], dd + w + 1))
                        own(e.tensor_tensor(chunked(kq[:, 1] if w == 0 else kn, i), plain(src), plain(t), ALU.mult))
                    settle()
                    e.tensor_tensor(chunked(kq[:, 0], i), chunked(kn, i), plain(qs[:, 4 + k2]), ALU.mult
                                    ).then_inc(S["dve_nrm"], 1)
                elif kind == "gram":
                    mk = mask[:, :, :].rearrange("p a t -> p (a t)").unsqueeze(1).to_broadcast([128, NCH, 64])
                    for h in range(H):
                        e.wait_ge(S["pe_d"], dd + h + 1)
                        e.tensor_tensor(alt[:, i, h].rearrange("p n a t -> p n (a t)"),
                                        ps_d[:, (dd + h) % NRING].rearrange("p (n x) -> p n x", n=NCH), mk, ALU.mult
                                        ).then_inc(S["dve_d"], 1)
                elif kind == "inverse":
                    e.wait_ge(S["dve_d"], dd)
                    e.wait_ge(S["eye_done"], i + 1)
                    at_a = alt[:, i, :, :, 0, :].rearrange("p h n t -> p t (h n)")
                    own(e.transpose(lmat[:, i].rearrange("p i j -> p (i j)"), at_a))
                    settle()
                    for j in range(DH - 1):
                        k = DH - 1 - j
                        sub = tinv[:, i, j + 1:DH, 0:j + 1]
                        prod = tmp[:, 0:k * (j + 1)].rearrange("p (i c) -> p i c", i=k)
                        own(e.tensor_tensor(prod, lmat[:, i, j + 1:DH, j:j + 1].to_broadcast([128, k, j + 1]),
                                            tinv[:, i, j:j + 1, 0:j + 1].to_broadcast([128, k, j + 1]), ALU.mult))
                        settle()
                        own(e.tensor_tensor(sub, sub, prod, ALU.subtract))
                        settle()
                    e.transpose(at_a, tinv[:, i].rearrange("p i j -> p (i j)")).then_inc(S["inv_done"], 1)
                    if i:
                        e.transpose(paths[4].rearrange("p t c -> p (t c)"),
                                    vpad[:, :, HIST:HIST + L].rearrange("p b (w t) -> p t b w", t=64)
                                    ).then_inc(S["path4"], 1)
                elif kind == "chain":
                    n = i
                    spread_u(n, 0)
                    if n < NCH - 1:
                        mask_s(n, 0)
                    spread_u(n, 1)
                    if n == 0:
                        e.wait_ge(S["st_zero"], 1)
                    if STAT_ORDER[n // 2] == 4:
                        e.wait_ge(S["path4"], 1)
                    sums(n)
                    if n < NCH - 1:
                        mask_s(n, 1)
                    absolute_sums(n)
                    square_sums(n)
                elif kind == "stats":
                    e.wait_ge(S["act_o"], 2 * NCH)
                    for half in range(2):
                        r = slice(32 * half, 32 * half + 32)
                        e.transpose(paths[3][:, r].rearrange("p t c -> p (t c)"),
                                    o_t[:, :].rearrange("p (x t) -> p t x", t=64)[:, r]).then_inc(S["path3"], 1)
                    e.wait_ge(S["path3"], 1)
                    sums(NCH)
                    absolute_sums(NCH)
                    square_sums(NCH)
                    e.wait_ge(S["path3"], 2)
                    sums(NCH + 1)
                    absolute_sums(NCH + 1)
                    turn_stats(0)
                    square_sums(NCH + 1)
                    turn_stats(1)
                elif kind == "logit":
                    if i == 0:
                        numbers()
                    e.wait_ge(S["pe_d"], dd + 1)
                    e.tensor_scalar(quarter(lg, i), ps_d[:, dd % NRING].rearrange("p (x t) -> p x t", t=16),
                                    vc("gb2"), vc("itau"), ALU.add, ALU.mult).then_inc(S["dve_d"], 1)
                elif kind == "soft":
                    r = slice(32 * i, 32 * i + 32)
                    e.wait_ge(S["dve_d"], dd)
                    own(e.transpose(pl[:, r].rearrange("p t c -> p (t c)"),
                                    lg[:, :].rearrange("p (x t) -> p t x", t=64)[:, r]))
                    settle()
                    lo5 = pl[:, r, 0:P]

                    def per_token(v):
                        return v.unsqueeze(2).to_broadcast([128, 32, P])

                    own(e.tensor_reduce(mx, lo5, AX_X, ALU.max))
                    settle()
                    e.tensor_tensor(ex5[:, i], lo5, per_token(mx), ALU.subtract).then_inc(S["dve_sub"], 1)
                    e.wait_ge(S["act_exp"], i + 1)
                    own(e.tensor_reduce(su, ex5[:, i], AX_X, ALU.add))
                    settle()
                    own(e.reciprocal(su, su))
                    settle()
                    own(e.tensor_tensor(pr5[:, i], ex5[:, i], per_token(su), ALU.mult))
                    settle()
                    e.scalar_tensor_tensor(out=pr5[:, i], in0=pr5[:, i], scalar=vc("rest"),
                                               in1=vc("eps", 0, P).unsqueeze(1).to_broadcast([128, 32, P]),
                                               op0=ALU.mult, op1=ALU.add).then_inc(S["probs"], 1)
                elif kind == "mix":
                    e.wait_ge(S["probs"], 1)
                    mixture(e, 0, MIX_SPLIT, own, settle).then_inc(S["mixed"], 1)
                elif kind == "scale":
                    r = slice(32 * i, 32 * i + 32)
                    e.wait_ge(S["act_osq"], i + 1)
                    own(e.tensor_reduce(ms, o_sq, AX_X, ALU.add))
                    settle()
                    e.tensor_scalar(var, ms, 1.0 / DH, RMS_EPS, ALU.mult, ALU.add).then_inc(S["dve_ms"], 1)
                    e.wait_ge(S["act_rms"], i + 1)
                    own(e.tensor_tensor(t2, rt, rt, ALU.mult))
                    settle()
                    own(e.scalar_tensor_tensor(out=t2, in0=t2, scalar=-0.5, in1=var, op0=ALU.mult, op1=ALU.mult))
                    settle()
                    own(e.scalar_tensor_tensor(out=rt, in0=t2, scalar=1.5, in1=rt, op0=ALU.add, op1=ALU.mult))
                    settle()
                    e.wait_ge(S["mixed"], 1)
                    e.wait_ge(S["mixed_p"], i + 1)
                    own(e.tensor_tensor(paths[0][:, r], paths[0][:, r], rt.unsqueeze(2).to_broadcast([128, 32, DH]),
                                        ALU.mult))
                    settle()
                    for q in (2 * i, 2 * i + 1):
                        if i:
                            e.wait_ge(S["pe_d"], D_AT[("wo", 2, q - 2)] + 1)
                        e.transpose(o_c[:, q % 2].rearrange("p (x t) -> p t x", t=16),
                                    paths[0][:, 16 * q:16 * q + 16].rearrange("p t c -> p (t c)")
                                    ).then_inc(S["o_turned"], 1)
                elif kind == "wo":
                    e.wait_ge(S["pe_d"], dd + 1)
                    e.tensor_tensor(quarter(x_t[:, :], i), quarter(x_t[:, :], i),
                                    ps_d[:, dd % NRING].rearrange("p (x t) -> p x t", t=16), ALU.add
                                    ).then_inc(S["dve_d"], 1)


_OUT = (B * L, D)


def lay_out(x):
    import numpy as np

    def cols(name):
        return np.asarray(x[name]).reshape(-1, 128).T

    a = {k: np.asarray(v) for k, v in x.items()}
    fir = np.zeros((D, 128, 3), np.float32)
    for n, k in enumerate(("fir_s", "fir_m", "fir_l")):
        w = a["L0_attn_" + k]
        fir[:, WIN - w.shape[1]:WIN, n] = w
    gw2 = np.zeros((2 * D, H, 32), np.float32)
    gw2[:, :, :P] = a["L0_attn_gW2"].reshape(2 * D, H, P)
    gb2 = np.zeros((H, 32), np.float32)
    gb2[:, :P] = a["L0_attn_gb2"].reshape(H, P)
    vec = [cols("L0_ffn_w1_s"), cols("L0_ffn_w2_s"), cols("L0_ffn_h1_s"), cols("L0_ffn_h2_s"), cols("L0_ffn_w3_s"),
           np.tile(a["L0_attn_norm_w"], H)[:, None], np.repeat(a["L0_attn_log_tau"], DH)[:, None],
           gb2.reshape(128, 1), cols("L0_attn_gb1"), np.repeat(a["L0_attn_eps_logit"], DH, axis=0)]
    taps = np.stack([a["L0_attn_conv_" + k].T for k in "qkv"]).reshape(1, 3 * TAPS * D)
    proj = [a["L0_attn_Wq"], a["L0_attn_Wk"], a["L0_attn_Wv"], np.repeat(a["L0_attn_Wb"], DH, axis=1)]
    out = {
        "x": a["L0_attn_hidden_states"].reshape(B * L, D),
        "w1": a["L0_ffn_w1_w"].T, "w2": a["L0_ffn_w2_w"].T, "h1": a["L0_ffn_h1_w"].T, "h2": a["L0_ffn_h2_w"].T,
        "w3": a["L0_ffn_w3_w"].T, "vec": np.concatenate(vec, axis=1), "proj": np.concatenate(proj, axis=1),
        "taps": taps, "fir": fir.reshape(4 * H, 8, 384).transpose(0, 2, 1).reshape(4 * H, 384 * 8), "gW1": a["L0_attn_gW1"], "gW2": gw2.reshape(2 * D, 128),
        "Wo": a["L0_attn_Wo"],
    }
    return {k: np.ascontiguousarray(v) for k, v in out.items()}


def kernel(**inputs):
    import concourse.bacc as bacc
    from concourse.bass_utils import run_bass_kernel_spmd

    nc = bacc.Bacc("TRN2", target_bir_lowering=False, num_devices=1)
    arrays = lay_out(inputs)
    d = {k: nc.dram_tensor("in_" + k, v.shape, mybir.dt.from_np(v.dtype), kind="ExternalInput").ap() for k, v in arrays.items()}
    out = nc.dram_tensor("y", _OUT, F32, kind="ExternalOutput").ap()
    program(nc, d, out)
    r = run_bass_kernel_spmd(nc, [{"in_" + k: v for k, v in arrays.items()}], core_ids=[0])
    return r.results[0]["y"].reshape(B, L, D)
```
